# Optimizing a Trainium2 kernel written in Bass

```python
import numpy as np
import jax
import jax.numpy as jnp

def _softmax(x, axis=-1):
    return jax.nn.softmax(x, axis=axis)

def _gelu(x):
    return jax.nn.gelu(x, approximate=True)

def _silu(x):
    return jax.nn.silu(x)

def _sigmoid(x):
    return jax.nn.sigmoid(x)

def _layernorm(x, axis=-1, eps=1e-05):
    m = jnp.mean(x, axis=axis, keepdims=True)
    v = jnp.var(x, axis=axis, keepdims=True)
    return (x - m) / jnp.sqrt(v + eps)

def _scatter_add(tgt, idx, src, axis=0):
    return tgt.at[idx].add(src)

def _segment_sum(src, seg, n):
    return jax.ops.segment_sum(src, seg, n)
kernel_name = 'mk_lm_tower_d1_tok_ids1024_r4_1a863f'

def setup_inputs(seed: int=0):
    np.random.seed(seed)
    _w = jnp.asarray

    def _rec_inputs():
        import jax
        import jax.numpy as jnp
        _rk = jax.random.key(seed)
        x = jax.random.randint(jax.random.fold_in(_rk, 1), (4, 512), 0, 256, jnp.int32)
        return x
    x = _rec_inputs()

    def _L0_tok_setup():
        import jax, jax.numpy as jnp
        import numpy as np
        B, T, V = (8, 512, 256)
        key = jax.random.key(seed)
        k1, k2, k3, k4, k5 = jax.random.split(key, 5)
        idx = jax.random.randint(k1, (B, T), 0, V)
        v = 0.02 * jax.random.normal(k2, (T, 1), dtype=jnp.float32)
        Wk = 0.02 * jax.random.normal(k3, (V, V), dtype=jnp.float32)
        Wq = 0.02 * jax.random.normal(k4, (V, V), dtype=jnp.float32)
        Wv = 0.02 * jax.random.normal(k5, (V, V), dtype=jnp.float32)
        return {'idx': idx, 'v': v, 'Wk': Wk, 'Wq': Wq, 'Wv': Wv}
    _L0_tok_all = _L0_tok_setup()
    _L0_tok_in = {k: v for k, v in _L0_tok_all.items() if k in ('v', 'Wk', 'Wq', 'Wv')}
    del _L0_tok_all

    def _L0_attn_setup():
        import jax, jax.numpy as jnp
        import numpy as np
        EMBED = 256
        HEADS = 16
        HEAD_DIM = EMBED // HEADS
        key = jax.random.key(seed)
        k1, k2, k3, k4, k5 = jax.random.split(key, 5)
        scale = 1.0 / np.sqrt(EMBED)
        return {'x': jax.random.normal(k1, (4, 512, EMBED), dtype=jnp.float32), 'qkv_w': jax.random.uniform(k2, (3 * EMBED, EMBED), minval=-scale, maxval=scale, dtype=jnp.float32), 'qkv_b': jax.random.uniform(k3, (3 * EMBED,), minval=-scale, maxval=scale, dtype=jnp.float32), 'out_w': jax.random.uniform(k4, (EMBED, EMBED), minval=-scale, maxval=scale, dtype=jnp.float32), 'out_b': jax.random.uniform(k5, (EMBED,), minval=-scale, maxval=scale, dtype=jnp.float32)}
    _L0_attn_all = _L0_attn_setup()
    _L0_attn_in = {k: v for k, v in _L0_attn_all.items() if k in ('qkv_w', 'qkv_b', 'out_w', 'out_b')}
    del _L0_attn_all

    def _L0_ffn_setup():
        import jax, jax.numpy as jnp
        import numpy as np
        LORA_DIM = 16
        LORA_TOKEN_INDEX = 1
        B, S, D, H = (4, 512, 256, 1024)
        key = jax.random.key(seed)
        ks = jax.random.split(key, 6)
        x = jax.random.normal(ks[0], (B, S, D), dtype=jnp.float32)
        W1 = jax.random.normal(ks[1], (H, D), dtype=jnp.float32) * 0.02
        b1 = jnp.zeros((H,), dtype=jnp.float32)
        W2 = jax.random.normal(ks[2], (D, H), dtype=jnp.float32) * 0.02
        b2 = jnp.zeros((D,), dtype=jnp.float32)
        scale = jnp.asarray(0.001, dtype=jnp.float32)
        return {'x': x, 'W1': W1, 'b1': b1, 'W2': W2, 'b2': b2, 'scale': scale}
    _L0_ffn_all = _L0_ffn_setup()
    _L0_ffn_in = {k: v for k, v in _L0_ffn_all.items() if k in ('W1', 'b1', 'W2', 'b2', 'scale')}
    del _L0_ffn_all
    return {'x': x, 'L0_tok_v': _L0_tok_in['v'], 'L0_tok_Wk': _L0_tok_in['Wk'], 'L0_tok_Wq': _L0_tok_in['Wq'], 'L0_tok_Wv': _L0_tok_in['Wv'], 'L0_attn_qkv_w': _L0_attn_in['qkv_w'], 'L0_attn_qkv_b': _L0_attn_in['qkv_b'], 'L0_attn_out_w': _L0_attn_in['out_w'], 'L0_attn_out_b': _L0_attn_in['out_b'], 'L0_ffn_W1': _L0_ffn_in['W1'], 'L0_ffn_b1': _L0_ffn_in['b1'], 'L0_ffn_W2': _L0_ffn_in['W2'], 'L0_ffn_b2': _L0_ffn_in['b2'], 'L0_ffn_scale': _L0_ffn_in['scale']}

def reference(x, L0_tok_v, L0_tok_Wk, L0_tok_Wq, L0_tok_Wv, L0_attn_qkv_w, L0_attn_qkv_b, L0_attn_out_w, L0_attn_out_b, L0_ffn_W1, L0_ffn_b1, L0_ffn_W2, L0_ffn_b2, L0_ffn_scale):
    import jax
    import jax.numpy as jnp

    def _L0_tok_ref(idx, v, Wk, Wq, Wv):
        import jax, jax.numpy as jnp
        import numpy as np
        B, T, V = (8, 512, 256)
        Tn = v.shape[0]
        Vn = Wk.shape[0]
        e = jax.nn.one_hot(idx, Vn, dtype=jnp.float32)
        pos = jnp.arange(Tn)
        rel = jnp.clip(pos[:, None] - pos[None, :], 0)
        pos_embd = jnp.tril(v[rel, 0])
        layer_one = jnp.einsum('ts,bsv->btv', pos_embd, e)
        K = layer_one @ Wk.T
        Q = e @ Wq.T
        attention = jnp.einsum('btv,bsv->bts', Q, K)
        causal = jnp.tril(jnp.ones((Tn, Tn), dtype=bool))
        masked_attention = jnp.where(causal, attention, 0.0)
        output = jnp.einsum('bts,bsv->btv', masked_attention, e @ Wv.T)
        logits = output + 0.001
        return logits

    def _L0_attn_ref(x, qkv_w, qkv_b, out_w, out_b):
        import jax, jax.numpy as jnp
        import numpy as np
        EMBED = 256
        HEADS = 16
        HEAD_DIM = EMBED // HEADS
        b, n, _ = x.shape
        qkv = (jnp.einsum('bne,fe->bnf', x, qkv_w) + qkv_b).reshape(b, n, 3, HEADS, HEAD_DIM)
        q, k, v = (qkv[:, :, 0], qkv[:, :, 1], qkv[:, :, 2])
        scores = jnp.einsum('bnhd,bmhd->bhnm', q, k) / jnp.sqrt(jnp.float32(HEAD_DIM))
        attn = jax.nn.softmax(scores, axis=-1)
        out = jnp.einsum('bhnm,bmhd->bnhd', attn, v).reshape(b, n, EMBED)
        return jnp.einsum('bne,fe->bnf', out, out_w) + out_b

    def _L0_ffn_ref(x, W1, b1, W2, b2, scale):
        import jax, jax.numpy as jnp
        import numpy as np
        LORA_DIM = 16
        LORA_TOKEN_INDEX = 1
        B, S, D, H = (4, 512, 256, 1024)
        Bx, Sx, Dx = x.shape
        Hx = W1.shape[0]
        lt = jax.lax.dynamic_slice_in_dim(x, LORA_TOKEN_INDEX, LORA_DIM, axis=1)
        even = lt[:, ::2, :]
        odd = lt[:, 1::2, :]
        m1 = (even[:, :4, :, None] * odd[:, :4, None, :]).reshape(Bx, Hx, Dx)
        m2 = (even[:, 4:, :, None] * odd[:, 4:, None, :]).reshape(Bx, Dx, Hx)
        h = jnp.einsum('bsd,hd->bsh', x, W1) + scale * jnp.einsum('bsd,bhd->bsh', x, m1) + b1
        h = jax.nn.gelu(h, approximate=False)
        out = jnp.einsum('bsh,oh->bso', h, W2) + scale * jnp.einsum('bsh,boh->bso', h, m2) + b2
        return out
    h = _L0_tok_ref(x, L0_tok_v, L0_tok_Wk, L0_tok_Wq, L0_tok_Wv)
    h = h + _L0_attn_ref(_layernorm(h, axis=-1), L0_attn_qkv_w, L0_attn_qkv_b, L0_attn_out_w, L0_attn_out_b)
    h = h + _L0_ffn_ref(_layernorm(h, axis=-1), L0_ffn_W1, L0_ffn_b1, L0_ffn_W2, L0_ffn_b2, L0_ffn_scale)
    return h

_drawn_inputs = setup_inputs


def setup_inputs(seed=0):
    import zlib

    import numpy as np

    out = dict(_drawn_inputs(seed))
    spreads = {'L0_ffn_b1': (0.0, 0.1), 'L0_ffn_b2': (0.0, 0.1)}
    factors = {}
    for name, (base, spread) in spreads.items():
        noise = np.random.default_rng([zlib.crc32(name.encode()), seed]).standard_normal(out[name].shape)
        drawn = base * np.exp(spread * noise) if base else spread * noise
        out[name] = jnp.asarray(drawn.astype(out[name].dtype))
    for name, factor in factors.items():
        out[name] = (out[name] * factor).astype(out[name].dtype)
    return out
```

```python
from contextlib import ExitStack

import numpy as np
import concourse.bass as bass
from concourse import mybir

F32 = mybir.dt.float32
F32R = mybir.dt.float32r
I32 = mybir.dt.int32
ALU = mybir.AluOpType
ACT = mybir.ActivationFunctionType
AX = mybir.AxisListType

P = 128
B, T = 4, 512
D = 256
HID = 1024
HEADS, HD = 16, 16
NT = T // P
ND = D // P
NH = HID // P
GH = 4
NG = HEADS // GH
GR = GH * HD
VW = 32
MAXROW = 96
STK = MAXROW + 2
EPS = 1e-5
RING = 3


def tower_kernel(nc, A):
    ctx = ExitStack()
    with ctx:
        def sb(name, shape, dt=F32):
            return ctx.enter_context(nc.sbuf_tensor(name, shape, dt))

        def sem(name):
            return ctx.enter_context(nc.semaphore(name))

        ident = sb("ident", [P, P])
        causal = sb("causal", [P, P])
        iota_free = sb("iota_free", [P, D])
        row_id = sb("row_id", [P, ND])
        select = sb("select", [P, 8, P])
        minus_half = sb("minus_half", [P, NT])
        toep = [sb(f"toep_{c}", [P, T], F32R) for c in "hl"]
        g_mat = [sb(f"g_mat_{c}", [P, ND, D], F32R) for c in "hl"]
        wvT = [sb(f"wvT_{c}", [P, ND, D], F32R) for c in "hl"]
        wqkvT = [sb(f"wqkvT_{c}", [P, ND, 3 * D], F32R) for c in "hl"]
        woT = [sb(f"woT_{c}", [P, ND, D], F32R) for c in "hl"]
        w1T = sb("w1T", [P, ND, HID])
        w2T = sb("w2T", [P, NH, D])
        qk_bias = sb("qk_bias", [P, 4])
        v_bias = sb("v_bias", [P, D])
        out_bias = sb("out_bias", [P, D])
        b1_col = sb("b1_col", [P, NH])
        b2_row = sb("b2_row", [P, D])
        scale = sb("scale", [P, 1])
        idx_row = sb("idx_row", [P, B * T], I32)
        idx_col_i = sb("idx_col_i", [P, B * NT], I32)
        idx_col = sb("idx_col", [P, B * NT])

        onehot = sb("onehot", [P, NT, D], F32R)
        onehotT = sb("onehotT", [P, ND, T], F32R)
        pool_a = sb("pool_a", [P, 8704], F32R)
        h = sb("h", [P, NT, D])
        xn = sb("xn", [P, NT, D])
        xT = [sb(f"xT_{c}", [P, ND, T], F32R) for c in "hl"]
        stats = sb("stats", [P, NT, 6])
        mean_var = sb("mean_var", [P, NT, 2])
        var_eps = sb("var_eps", [P, NT])
        rstd = sb("rstd", [P, NT])
        k_stack = sb("k_stack", [P, 2, GH * T], F32R)
        q_stack = sb("q_stack", [P, 2, GH * T], F32R)
        v_ext = sb("v_ext", [P, NT, HEADS, VW])
        probs = sb("probs", [P, 8192])
        row_max = sb("row_max", [P, 2, GH * NT])
        neg_max = [sb(f"neg_max_{c}", [GH * NT, 2, P], F32R) for c in "hl"]
        attT = sb("attT", [P, T])
        inv_sum = sb("inv_sum", [P, NT, GH])
        odd_scaled = sb("odd_scaled", [P, ND, 8])
        hidT = [sb(f"hidT_{c}", [P, RING, T], F32R) for c in "hl"]

        def cut(at, *shape):
            n = int(np.prod(shape))
            names = " ".join(f"d{i}" for i in range(len(shape)))
            sizes = {f"d{i}": s for i, s in enumerate(shape[1:], 1)}
            v = pool_a[:, at:at + n]
            return v if len(shape) == 1 else v.rearrange(f"p ({names}) -> p {names}", **sizes)

        mixT = [cut(0, ND, T), cut(1024, ND, T)]
        qgT = [cut(2048, ND, T), cut(3072, ND, T)]
        ev = cut(4096, NT, 2, D)
        tri = [k * T - P * (k * (k - 1) // 2) for k in range(NT)]
        att = [cut(6144, 1280), cut(6144 + 1280, 1280)]
        qk = [cut(0, 4, T), cut(2048, 4, T)]
        w1_now = [cut(0, ND, HID), cut(2048, ND, HID)]
        w2_now = [cut(4096, NH, D), cut(6144, NH, D)]

        probs_ring = probs[:, :].rearrange("p (u h m n) -> p u h m n", u=2, h=GH, m=2)
        w1_full = probs[:, 0:2048].rearrange("p (j n) -> p j n", j=ND)
        w2_full = probs[:, 2048:4096].rearrange("p (k n) -> p k n", k=NH)
        gelu = probs[:, 4096:8192].rearrange("p (k n) -> p k n", k=NH)
        wstage = probs[:, :]

        def pb(name, shape):
            return ctx.enter_context(nc.psum_tensor(name, shape, F32))

        pair = [pb("pair0", [P, 2, T]), pb("pair1", [P, 2, T])]
        duo = pb("duo", [P, 2, T])
        solo = [pb("solo0", [P, T]), pb("solo1", [P, T])]
        bank = [pair[0][:, 0, :], pair[0][:, 1, :], pair[1][:, 0, :], pair[1][:, 1, :],
                duo[:, 0, :], duo[:, 1, :], solo[0][:, :], solo[1][:, :]]

        loaded = sem("loaded")
        w_loaded = [sem(f"w_loaded{i}") for i in range(4)]
        consts = sem("consts")
        split_h, split_l = sem("split_h"), sem("split_l")
        g_made, g_split_h = sem("g_made"), sem("g_split_h")
        v_set, stacks_set = sem("v_set"), sem("stacks_set")
        idx_ready = sem("idx_ready")
        S = {n: sem(n) for n in (
            "onehot_made", "qg_sum", "mix_sum", "ev_sum", "qg_h", "qg_l", "mix_h", "mix_l", "ev_act", "ev_dve",
            "att_sum", "att_masked", "att_h", "att_l", "tok_sum", "h_made",
            "eps_added", "rstd_made", "xn_made", "turned", "xT_h", "xT_l", "odd_made",
            "qk_sum", "qk_h", "qk_l", "v_sum", "v_made",
            "scores", "reduced", "max_turned", "max_h", "max_l",
            "scoresT", "exped", "pv_done", "attT_made", "att_turned", "recip", "att_out",
            "bias_added", "proj_sum", "resid", "b2_added", "bcast",
            "w1_made", "w1_h", "w1_l", "w2_made", "w2_h", "w2_l",
            "hid_sum", "gelu_made", "hid_h", "hid_l", "hid_used", "out_made")}
        stack_in = [sem("stack_in0"), sem("stack_in1")]
        max_in = [sem("max_in0"), sem("max_in1")]
        h_free = sem("h_free")

        def seq_waits(eng, b, count):
            def wait(name, k):
                eng.wait_ge(S[name], b * count[name] + k)
            return wait

        COUNT = dict(
            onehot_made=6, qg_sum=4, mix_sum=2, ev_sum=4, qg_h=2, qg_l=2, mix_h=2, mix_l=2, ev_act=2, ev_dve=2,
            att_sum=4, att_masked=4, att_h=4, att_l=4, tok_sum=4, h_made=4,
            eps_added=2, rstd_made=2, xn_made=8, turned=6, xT_h=6, xT_l=6, odd_made=2,
            qk_sum=4, qk_h=4, qk_l=4, v_sum=2, v_made=4,
            scores=64, reduced=64, max_turned=4, max_h=4, max_l=4,
            scoresT=32, exped=32, pv_done=8, attT_made=4, att_turned=4, recip=4, att_out=4,
            bias_added=4, proj_sum=4, resid=4, b2_added=4, bcast=4,
            w1_made=4, w1_h=4, w1_l=4, w2_made=2, w2_h=2, w2_l=2,
            hid_sum=8, gelu_made=8, hid_h=8, hid_l=8, hid_used=8, out_made=4)

        def f32(ap):
            return ap.bitcast(F32)

        SPLITS = [(toep, 0, T, 0), (wvT, T, ND * D, 0), (wqkvT, 1024, ND * 3 * D, 1), (woT, 2560, ND * D, 1)]

        def flat(t):
            v = t[:]
            return v if len(v.shape) == 2 else v.rearrange("p a b -> p (a b)")

        block = ctx.enter_context(nc.Block())

        @block.sync
        def _(sp):
            sp.dma_start(wstage[:, 3072:3584].rearrange("p (k n) -> p k n", k=ND),
                         A["wq"].rearrange("(k p) n -> p k n", p=P)).then_inc(w_loaded[2], 16)
            sp.dma_start(wstage[:, 3584:4096].rearrange("p (k n) -> p k n", k=ND),
                         A["wk"].rearrange("(k p) n -> p k n", p=P)).then_inc(w_loaded[2], 16)
            sp.dma_start(wstage[:, 0:T], bass.AP(A["v_pad"].tensor, 0, [[1, P], [1, T]])).then_inc(w_loaded[0], 16)
            sp.dma_start(wstage[:, T:1024].rearrange("p (k n) -> p k n", k=ND),
                         A["wvT"].rearrange("(k p) n -> p k n", p=P)).then_inc(w_loaded[0], 16)
            sp.dma_start(idx_col_i[:, :], A["idx_cols"]).then_inc(loaded, 16)
            sp.dma_start(idx_row[:, :], A["idx"].partition_broadcast(P)).then_inc(loaded, 16)
            sp.dma_start(wstage[:, 1024:2560].rearrange("p (k n) -> p k n", k=ND),
                         A["wqkvT"].rearrange("(k p) n -> p k n", p=P)).then_inc(w_loaded[1], 16)
            sp.dma_start(wstage[:, 2560:3072].rearrange("p (k n) -> p k n", k=ND),
                         A["woT"].rearrange("(k p) n -> p k n", p=P)).then_inc(w_loaded[1], 16)
            sp.dma_start(qk_bias[:, :], A["qk_bias"]).then_inc(loaded, 16)
            sp.dma_start(v_bias[:, :], A["v_bias"].partition_broadcast(P)).then_inc(loaded, 16)
            sp.dma_start(out_bias[:, :], A["out_bias"].partition_broadcast(P)).then_inc(loaded, 16)
            sp.dma_start(b1_col[:, :], A["b1_col"]).then_inc(loaded, 16)
            sp.dma_start(b2_row[:, :], A["b2"].partition_broadcast(P)).then_inc(loaded, 16)
            sp.dma_start(scale[:, :], A["scale"].partition_broadcast(P)).then_inc(loaded, 16)
            sp.dma_start(w1T[:, :, :], A["w1T"].rearrange("(k p) n -> p k n", p=P)).then_inc(loaded, 16)
            sp.dma_start(w2T[:, :, :], A["w2T"].rearrange("(k p) n -> p k n", p=P)).then_inc(loaded, 16)
            sp.sem_inc(h_free, 1)
            sp.wait_ge(stacks_set, 1)
            with sp.Fori(0, B) as b:
                wait = seq_waits(sp, b, COUNT)

                def stack(g):
                    fb, at = g // 2, GR * (g % 2)
                    for dst, f, parts in ((k_stack, 2 + fb, (0, 1, 0)), (q_stack, fb, (0, 0, 1))):
                        for slot, part in enumerate(parts):
                            sp.dma_start(f32(dst[HD * slot:HD * (slot + 1), g % 2, :]),
                                         f32(qk[part][at:at + GR, f, :])).then_inc(stack_in[g % 2], 16)

                def stack_max(g):
                    wait("max_h", g + 1)
                    wait("max_l", g + 1)
                    for part in range(2):
                        sp.dma_start(f32(q_stack[MAXROW + part:MAXROW + part + 1, g % 2, :]),
                                     f32(neg_max[part][:, g % 2, :])).then_inc(max_in[g % 2], 16)

                wait("qk_h", 2)
                wait("qk_l", 2)
                stack(0)
                stack(1)
                stack_max(0)
                wait("qk_h", 4)
                wait("qk_l", 4)
                for g in range(NG - 1):
                    stack_max(g + 1)
                    if g + 2 < NG:
                        wait("scoresT", 8 * (g + 1))
                        stack(g + 2)
                for i in range(NT):
                    wait("out_made", i + 1)
                    sp.dma_start(A["out"][b, P * i:P * (i + 1), :], h[:, i, :]).then_inc(h_free, 16)
            sp.wait_ge(h_free, 64 * B + 1)

        @block.gpsimd
        def _(pool):
            pool.memset(ident[:, :], 0.0).then_inc(consts, 1)
            pool.memset(causal[:, :], 1.0).then_inc(consts, 1)
            pool.memset(select[:, :, :], 0.0).then_inc(consts, 1)
            pool.memset(minus_half[:, :], -0.5).then_inc(consts, 1)
            pool.iota(iota_free[:, :], [[1, D]], base=0, channel_multiplier=0,
                      allow_small_or_imprecise_dtypes=True).then_inc(consts, 1)
            pool.iota(row_id[:, :], [[P, ND]], base=0, channel_multiplier=1,
                      allow_small_or_imprecise_dtypes=True).then_inc(consts, 1)
            pool.wait_ge(consts, 6)
            pool.affine_select(out=ident[:, :], in_=ident[:, :], compare_op=ALU.not_equal, fill=1.0,
                               base=0, pattern=[[-1, P]], channel_multiplier=1).then_inc(consts, 1)
            pool.affine_select(out=causal[:, :], in_=causal[:, :], compare_op=ALU.is_ge, fill=0.0,
                               base=0, pattern=[[1, P]], channel_multiplier=-1).then_inc(consts, 1)
            pool.affine_select(out=select[:, :, :], in_=select[:, :, :], compare_op=ALU.not_equal, fill=1.0,
                               base=-1, pattern=[[-2, 8], [0, P]], channel_multiplier=1).then_inc(consts, 1)
            for n, (dst, at, width, load) in enumerate(SPLITS):
                pool.wait_ge(w_loaded[load], 32)
                pool.tensor_scalar(flat(dst[0]), wstage[:, at:at + width], 1.0, 0.0, ALU.mult, ALU.add)\
                    .then_inc(split_h, 1)
            pool.memset(v_ext[:, :, :, HD:VW], 0.0).then_inc(v_set, 1)
            pool.wait_ge(v_set, 1)
            pool.memset(v_ext[:, :, :, HD:HD + 1], 1.0).then_inc(v_set, 1)
            with pool.Fori(0, B) as b:
                wait = seq_waits(pool, b, COUNT)

                def inverse_std(n):
                    wait("eps_added", n + 1)
                    pool.tensor_tensor(rstd[:, :], var_eps[:, :], minus_half[:, :], ALU.pow)\
                        .then_inc(S["rstd_made"], 1)

                inverse_std(0)
                wait("xn_made", NT)
                for i in range(NT):
                    pool.tensor_tensor(h[:, i, :], h[:, i, :], out_bias[:, :], ALU.add)\
                        .then_inc(S["bias_added"], 1)
                inverse_std(1)
                wait("xn_made", 2 * NT)
                for i in range(NT):
                    pool.tensor_tensor(h[:, i, :], h[:, i, :], b2_row[:, :], ALU.add)\
                        .then_inc(S["b2_added"], 1)

        @block.scalar
        def _(act):
            for j in range(ND):
                act.wait_ge(g_made, j + 1)
                act.activation(g_mat[0][:, j, :], bank[j][:, 0:D], ACT.Copy).then_inc(g_split_h, 1)
            with act.Fori(0, B) as b:
                wait = seq_waits(act, b, COUNT)

                def turned_high(n):
                    for j in range(ND):
                        wait("turned", ND * n + j + 1)
                        act.activation(xT[0][:, j, :], bank[(2, 4, 2)[n] + j], ACT.Copy).then_inc(S["xT_h"], 1)

                for j in range(ND):
                    wait("qg_sum", 2 * j + 1)
                    act.activation(qgT[0][:, j, :], bank[2 * j], ACT.Copy).then_inc(S["qg_h"], 1)
                for j in range(ND):
                    wait("mix_sum", j + 1)
                    act.activation(mixT[0][:, j, :], bank[4 + j], ACT.Copy).then_inc(S["mix_h"], 1)
                for n, i in enumerate((0, 2)):
                    wait("ev_sum", i + 1)
                    act.activation(ev[:, i, :, :], bank[(6, 7, 0, 1)[i]], ACT.Copy).then_inc(S["ev_act"], 1)
                for k in range(NT):
                    wait("att_masked", k + 1)
                    act.activation(att[0][:, tri[k]:tri[k] + T - P * k], bank[2 + k][:, P * k:T], ACT.Copy)\
                        .then_inc(S["att_h"], 1)
                act.wait_ge(h_free, b * 64 + 1)
                for i in range(NT):
                    wait("tok_sum", i + 1)
                    act.activation(h[:, i, :], bank[(6, 7, 0, 1)[i]][:, 0:D], ACT.Copy, bias=0.001)\
                        .then_inc(S["h_made"], 1)
                turned_high(0)
                for n, f in enumerate((2, 0, 3, 1)):
                    wait("qk_sum", n + 1)
                    act.activation(qk[0][:, f, :], bank[(0, 1, 6, 7)[n]], ACT.Identity, bias=qk_bias[:, f:f + 1])\
                        .then_inc(S["qk_h"], 1)

                def max_high(g):
                    wait("max_turned", g + 1)
                    act.activation(neg_max[0][:, g % 2, :], bank[7][0:GH * NT, 0:P], ACT.Copy, scale=-1.0)\
                        .then_inc(S["max_h"], 1)

                max_high(0)
                for g in range(NG):
                    for half in range(2):
                        u = 2 * g + half
                        for i in range(GH):
                            n = GH * u + i
                            wait("scoresT", n + 1)
                            if u >= 2 and i == 0:
                                wait("pv_done", u - 1)
                            act.activation(probs_ring[:, u % 2, i, :, :], pair[n % 2][:, :, :], ACT.Exp,
                                           scale=float(HD) ** -0.5).then_inc(S["exped"], 1)
                            if half == 0 and i == 3 and g >= 1:
                                wait("pv_done", 2 * g)
                                act.activation(attT[:, :], bank[6], ACT.Copy).then_inc(S["attT_made"], 1)
                    if g + 1 < NG:
                        max_high(g + 1)
                wait("pv_done", 2 * NG)
                act.activation(attT[:, :], bank[6], ACT.Copy).then_inc(S["attT_made"], 1)
                turned_high(1)
                turned_high(2)
                for i in range(4):
                    wait("w1_made", i + 1)
                    cols = slice(D * i, D * (i + 1))
                    act.activation(w1_now[0][:, :, cols], w1_full[:, :, cols], ACT.Copy).then_inc(S["w1_h"], 1)
                for j in range(ND):
                    wait("w2_made", j + 1)
                    act.activation(w2_now[0][:, j::ND, :], w2_full[:, j::ND, :], ACT.Copy).then_inc(S["w2_h"], 1)

                def hidden_high(k):
                    if k >= RING:
                        wait("hid_used", k - RING + 1)
                    act.wait_ge(S["gelu_made"], b * NH + k + 1)
                    act.activation(hidT[0][:, k % RING, :], gelu[:, k, :], ACT.Copy).then_inc(S["hid_h"], 1)

                for k in range(NH):
                    wait("hid_sum", k + 1)
                    act.activation(gelu[:, k, :], bank[2 + k % 4], ACT.Gelu, bias=b1_col[:, k:k + 1])\
                        .then_inc(S["gelu_made"], 1)
                    if k:
                        hidden_high(k - 1)
                hidden_high(NH - 1)

        @block.vector
        def _(dve):
            for t in (k_stack, q_stack):
                dve.memset(f32(t[32:64, :, :]), 0.0)
                dve.memset(f32(t[64:96, :, :]), 0.0)
            dve.memset(f32(k_stack[MAXROW:STK, :, :]), 1.0).then_inc(stacks_set, 1)
            dve.wait_ge(loaded, 16 * 10)
            dve.tensor_copy(idx_col[:, :], idx_col_i[:, :]).then_inc(idx_ready, 1)
            for n, (dst, at, width, load) in enumerate(SPLITS):
                dve.wait_ge(split_h, n + 1)
                dve.tensor_tensor(flat(dst[1]), wstage[:, at:at + width], f32(flat(dst[0])), ALU.subtract)\
                    .then_inc(split_l, 1)
            for j in range(ND):
                dve.wait_ge(g_split_h, j + 1)
                dve.tensor_tensor(g_mat[1][:, j, :], bank[j][:, 0:D], f32(g_mat[0][:, j, :]), ALU.subtract)\
                    .then_inc(split_l, 1)
            dve.wait_ge(idx_ready, 1)
            dve.wait_ge(consts, 9)
            with dve.Fori(0, B) as b:
                wait = seq_waits(dve, b, COUNT)

                def norm(n):
                    for i in range(NT):
                        wait("resid" if n else "h_made", i + 1)
                        dve.bn_stats(stats[:, i, :], h[:, i, :])
                    dve.drain()
                    for i in range(NT):
                        dve.bn_aggr(mean_var[:, i, :], stats[:, i, :])
                    dve.drain()
                    dve.tensor_scalar(var_eps[:, :], mean_var[:, :, 1], EPS, None, ALU.add)\
                        .then_inc(S["eps_added"], 1)
                    wait("rstd_made", n + 1)
                    for i in range(NT):
                        dve.tensor_scalar(xn[:, i, :], h[:, i, :], mean_var[:, i, 0:1], rstd[:, i:i + 1],
                                          ALU.subtract, ALU.mult).then_inc(S["xn_made"], 1)

                def turned_low(n):
                    for j in range(ND):
                        wait("xT_h", ND * n + j + 1)
                        dve.tensor_tensor(xT[1][:, j, :], bank[(2, 4, 2)[n] + j], f32(xT[0][:, j, :]),
                                          ALU.subtract).then_inc(S["xT_l"], 1)

                for k in range(ND):
                    dve.tensor_scalar(onehotT[:, k, :], idx_row[:, bass.ds(b * T, T)], row_id[:, k:k + 1], None,
                                      ALU.is_equal).then_inc(S["onehot_made"], 1)
                for i in range(NT):
                    dve.tensor_scalar(onehot[:, i, :], iota_free[:, :], idx_col[:, bass.ds(b * NT + i, 1)], None,
                                      ALU.is_equal).then_inc(S["onehot_made"], 1)
                for j in range(ND):
                    wait("qg_sum", 2 * j + 2)
                    dve.tensor_copy(qgT[1][:, j, :], bank[2 * j + 1]).then_inc(S["qg_l"], 1)
                for j in range(ND):
                    wait("mix_h", j + 1)
                    dve.tensor_tensor(mixT[1][:, j, :], bank[4 + j], f32(mixT[0][:, j, :]), ALU.subtract)\
                        .then_inc(S["mix_l"], 1)
                for n, i in enumerate((1, 3)):
                    wait("ev_sum", i + 1)
                    dve.tensor_copy(ev[:, i, :, :], bank[(6, 7, 0, 1)[i]]).then_inc(S["ev_dve"], 1)

                def att_low(k):
                    wait("att_h", k + 1)
                    cols = slice(tri[k], tri[k] + T - P * k)
                    dve.tensor_tensor(att[1][:, cols], bank[2 + k][:, P * k:T], f32(att[0][:, cols]),
                                      ALU.subtract).then_inc(S["att_l"], 1)

                for k in range(NT):
                    wait("att_sum", k + 1)
                    diag = bank[2 + k][:, P * k:P * (k + 1)]
                    dve.tensor_tensor(diag, diag, causal[:, :], ALU.mult).then_inc(S["att_masked"], 1)
                    if k:
                        att_low(k - 1)
                att_low(NT - 1)
                norm(0)
                turned_low(0)
                for n, f in enumerate((2, 0, 3, 1)):
                    wait("qk_h", n + 1)
                    dve.scalar_tensor_tensor(out=qk[1][:, f, :], in0=bank[(0, 1, 6, 7)[n]],
                                             scalar=qk_bias[:, f:f + 1], in1=f32(qk[0][:, f, :]),
                                             op0=ALU.add, op1=ALU.subtract).then_inc(S["qk_l"], 1)
                for i in range(NT):
                    wait("v_sum", i // 2 + 1)
                    dve.tensor_tensor(
                        v_ext[:, i, :, 0:HD],
                        bank[4 + i // 2][:, D * (i % 2):D * (i % 2 + 1)].rearrange("p (h d) -> p h d", d=HD),
                        v_bias[:, :].rearrange("p (h d) -> p h d", d=HD), ALU.add).then_inc(S["v_made"], 1)

                def max_of(n):
                    g = n // (GH * NT)
                    at = n % (GH * NT)
                    wait("scores", n + 1)
                    dve.reduce_max(row_max[:, g % 2, at:at + 1], bank[4 + n % 2], axis=AX.X)\
                        .then_inc(S["reduced"], 1)

                def max_low(g):
                    wait("max_h", g + 1)
                    dve.scalar_tensor_tensor(out=neg_max[1][:, g % 2, :], in0=bank[7][0:GH * NT, 0:P], scalar=-1.0,
                                             in1=f32(neg_max[0][:, g % 2, :]), op0=ALU.mult, op1=ALU.subtract)\
                        .then_inc(S["max_l"], 1)

                def normalise(g):
                    wait("att_turned", g + 1)
                    o = bank[7].rearrange("p (n h w) -> p n h w", n=NT, h=GH)
                    dve.reciprocal(inv_sum[:, :, :], o[:, :, :, HD]).then_inc(S["recip"], 1)
                    wait("recip", g + 1)
                    dve.tensor_tensor(
                        xn[:, :, GR * g:GR * (g + 1)].rearrange("p n (h d) -> p n h d", h=GH), o[:, :, :, 0:HD],
                        inv_sum[:, :, :].unsqueeze(3).broadcast_to([P, NT, GH, HD]), ALU.mult)\
                        .then_inc(S["att_out"], 1)

                def w1_low(i):
                    wait("w1_h", i + 1)
                    cols = slice(D * i, D * (i + 1))
                    dve.tensor_tensor(w1_now[1][:, :, cols], w1_full[:, :, cols], f32(w1_now[0][:, :, cols]),
                                      ALU.subtract).then_inc(S["w1_l"], 1)

                MG = GH * NT
                for n in range(MG):
                    max_of(n)
                max_low(0)
                for g in range(NG):
                    for n in range(MG):
                        if g + 1 < NG:
                            max_of(MG * (g + 1) + n)
                        if n == 11 and g >= 1:
                            normalise(g - 1)
                    if g + 1 < NG:
                        max_low(g + 1)
                normalise(NG - 1)
                turned_low(1)
                for i in range(NT):
                    wait("bias_added", i + 1)
                    wait("proj_sum", i + 1)
                    dve.tensor_tensor(h[:, i, :], bank[i][:, 0:D], h[:, i, :], ALU.add).then_inc(S["resid"], 1)
                norm(1)
                turned_low(2)
                for j in range(ND):
                    dve.tensor_scalar(odd_scaled[:, j, :], bank[2 + j][:, 2:18:2], scale[:, 0:1], None, ALU.mult)\
                        .then_inc(S["odd_made"], 1)
                wait("odd_made", ND)
                for i in range(4):
                    wait("bcast", i // 2 + 1)
                    for j in range(ND):
                        last = dve.scalar_tensor_tensor(
                            out=w1_full[:, j, D * i:D * (i + 1)], in0=bank[6 + i // 2][:, D * (i % 2):D * (i % 2 + 1)],
                            scalar=odd_scaled[:, j, i:i + 1], in1=w1T[:, j, D * i:D * (i + 1)],
                            op0=ALU.mult, op1=ALU.add)
                    last.then_inc(S["w1_made"], 1)
                    if i:
                        w1_low(i - 1)
                w1_low(3)
                for j in range(ND):
                    for i in range(4):
                        wait("bcast", 2 + i // 2 + 1)
                        last = dve.scalar_tensor_tensor(
                            out=w2_full[:, j::ND, 64 * i:64 * (i + 1)],
                            in0=bank[i // 2][:, D * (i % 2):D * (i % 2 + 1)].rearrange("p (q r) -> p r q", r=4),
                            scalar=odd_scaled[:, j, 4 + i:5 + i], in1=w2T[:, j::ND, 64 * i:64 * (i + 1)],
                            op0=ALU.mult, op1=ALU.add)
                    last.then_inc(S["w2_made"], 1)
                for j in range(ND):
                    wait("w2_h", j + 1)
                    dve.tensor_tensor(w2_now[1][:, j::ND, :], w2_full[:, j::ND, :], f32(w2_now[0][:, j::ND, :]),
                                      ALU.subtract).then_inc(S["w2_l"], 1)
                for k in range(NH):
                    wait("hid_h", k + 1)
                    if k >= RING:
                        wait("hid_used", k - RING + 1)
                    dve.tensor_tensor(hidT[1][:, k % RING, :], gelu[:, k, :], f32(hidT[0][:, k % RING, :]),
                                      ALU.subtract).then_inc(S["hid_l"], 1)
                for i in range(NT):
                    wait("b2_added", i + 1)
                    wait("hid_used", NH)
                    dve.tensor_tensor(h[:, i, :], bank[(0, 1, 6, 7)[i]][:, 0:D], h[:, i, :], ALU.add)\
                        .then_inc(S["out_made"], 1)

        @block.tensor
        def _(pe):
            def split_product(out, lhs, rhs, inner):
                passes = [(k, a, c) for k in range(inner) for a, c in ((0, 0), (0, 1), (1, 0))]
                for n, (k, a, c) in enumerate(passes):
                    last = pe.matmul(out, lhs(a, k), rhs(c, k), start=(n == 0), stop=(n == len(passes) - 1))
                return last

            wq = wstage[:, 3072:3584].rearrange("p (k n) -> p k n", k=ND)
            wk = wstage[:, 3584:4096].rearrange("p (k n) -> p k n", k=ND)
            pe.wait_ge(w_loaded[2], 32)
            for j in range(ND):
                for k in range(ND):
                    last = pe.matmul(bank[j][:, 0:D], wq[:, k, P * j:P * (j + 1)], wk[:, k, :],
                                     start=(k == 0), stop=(k == ND - 1))
                last.then_inc(g_made, 1)
            pe.wait_ge(split_l, len(SPLITS) + ND)
            pe.wait_ge(consts, 9)
            pe.wait_ge(v_set, 2)
            with pe.Fori(0, B) as b:
                wait = seq_waits(pe, b, COUNT)
                wait("onehot_made", 2)
                for j in range(ND):
                    for part in range(2):
                        for k in range(ND):
                            last = pe.matmul(bank[2 * j + part], g_mat[part][:, k, P * j:P * (j + 1)],
                                             onehotT[:, k, :], start=(k == 0), stop=(k == ND - 1))
                        last.then_inc(S["qg_sum"], 1)
                wait("onehot_made", 6)
                for j in range(ND):
                    for part in range(2):
                        for k in range(NT):
                            last = pe.matmul(bank[4 + j][:, P * k:T], onehot[:, k, P * j:P * (j + 1)],
                                             toep[part][:, 0:T - P * k], start=(part == 0 and k == 0),
                                             stop=(part == 1 and k == NT - 1))
                    last.then_inc(S["mix_sum"], 1)
                for i in range(NT):
                    if i == 2:
                        wait("qg_h", 1)
                    if i == 3:
                        wait("qg_l", 1)
                    for part in range(2):
                        for k in range(ND):
                            last = pe.matmul(bank[(6, 7, 0, 1)[i]][:, D * part:D * (part + 1)],
                                             onehotT[:, k, P * i:P * (i + 1)], wvT[part][:, k, :],
                                             start=(k == 0), stop=(k == ND - 1))
                    last.then_inc(S["ev_sum"], 1)
                wait("qg_h", 2)
                wait("qg_l", 2)
                wait("mix_h", 2)
                wait("mix_l", 2)
                for k in range(NT):
                    split_product(bank[2 + k][:, P * k:T], lambda a, j: mixT[a][:, j, P * k:P * (k + 1)],
                                  lambda c, j: qgT[c][:, j, P * k:T], ND).then_inc(S["att_sum"], 1)
                wait("ev_act", 2)
                wait("ev_dve", 2)
                for i in range(NT):
                    wait("att_h", i + 1)
                    wait("att_l", i + 1)
                    split_product(bank[(6, 7, 0, 1)[i]][:, 0:D],
                                  lambda a, k: att[a][:, tri[k] + P * (i - k):tri[k] + P * (i - k + 1)],
                                  lambda c, k: ev[:, k, c, :], i + 1).then_inc(S["tok_sum"], 1)

                def turn(n):
                    for j in range(ND):
                        for i in range(NT):
                            last = pe.transpose(bank[(2, 4, 2)[n] + j][:, P * i:P * (i + 1)],
                                                xn[:, i, P * j:P * (j + 1)], ident[:, :])
                        last.then_inc(S["turned"], 1)
                    
                wait("xn_made", NT)
                turn(0)
                wait("xT_h", ND)
                wait("xT_l", ND)
                for n, f in enumerate((2, 0, 3, 1)):
                    split_product(bank[(0, 1, 6, 7)[n]], lambda a, k: wqkvT[a][:, k, P * f:P * (f + 1)],
                                  lambda c, k: xT[c][:, k, :], ND).then_inc(S["qk_sum"], 1)
                for i in range(NT):
                    last = split_product(bank[4 + i // 2][:, D * (i % 2):D * (i % 2 + 1)],
                                         lambda a, k: xT[a][:, k, P * i:P * (i + 1)],
                                         lambda c, k: wqkvT[c][:, k, 2 * D:3 * D], ND)
                    if i % 2:
                        last.then_inc(S["v_sum"], 1)

                def scores_for_max(n):
                    g, hd, i = n // (GH * NT), n // NT % GH, n % NT
                    if n < 2:
                        wait("v_made", 2 * n + 2)
                    else:
                        wait("reduced", n - 1)
                    if n % (GH * NT) == 0:
                        pe.wait_ge(stack_in[g % 2], b * 192 + 96 * (g // 2 + 1))
                    at = T * hd
                    pe.matmul(bank[4 + n % 2], q_stack[0:80, g % 2, at + P * i:at + P * (i + 1)],
                              k_stack[0:80, g % 2, at:at + T], start=True, stop=True).then_inc(S["scores"], 1)

                def turn_max(g):
                    wait("reduced", GH * NT * (g + 1))
                    if g == 0:
                        wait("qk_h", 4)
                        wait("qk_l", 4)
                    elif g == 1:
                        wait("max_l", 1)
                    else:
                        wait("att_out", g - 1)
                    pe.transpose(bank[7][0:GH * NT, 0:P], row_max[:, g % 2, :], ident[:, :])\
                        .then_inc(S["max_turned"], 1)

                def scoresT_pair(u, i):
                    g, half, n = u // 2, u % 2, GH * u + i
                    if half == 0 and i == 0:
                        pe.wait_ge(max_in[g % 2], b * 64 + 32 * (g // 2 + 1))
                    if n >= 2:
                        wait("exped", n - 1)
                    for m in range(2):
                        at = T * i + P * (2 * half + m)
                        last = pe.matmul(pair[n % 2][:, m, :], k_stack[0:STK, g % 2, at:at + P],
                                         q_stack[0:STK, g % 2, T * i:T * (i + 1)], start=True, stop=True)
                    last.then_inc(S["scoresT"], 1)

                def weigh_values(u, m):
                    g, half = u // 2, u % 2
                    if m == 0:
                        wait("exped", GH * (u + 1))
                        if half == 0 and g >= 1:
                            wait("attT_made", g)
                    for i in range(GH):
                        last = pe.matmul(bank[6][VW * i:VW * (i + 1), :], v_ext[:, 2 * half + m, GH * g + i, :],
                                         probs_ring[:, u % 2, i, m, :], start=(half == 0 and m == 0),
                                         stop=(half == 1 and m == 1))
                    if m == 1:
                        last.then_inc(S["pv_done"], 1)

                def turn_out(g):
                    wait("attT_made", g + 1)
                    if g + 1 < NG:
                        wait("max_l", g + 2)
                    else:
                        wait("att_out", g)
                    for i in range(NT):
                        last = pe.transpose(bank[7][:, P * i:P * (i + 1)], attT[:, P * i:P * (i + 1)], ident[:, :])
                    last.then_inc(S["att_turned"], 1)

                MG = GH * NT
                for n in range(MG):
                    scores_for_max(n)
                turn_max(0)
                for u in range(2 * NG):
                    g, half = u // 2, u % 2
                    for i in range(GH):
                        scoresT_pair(u, i)
                        if g + 1 < NG:
                            for n in range(2):
                                scores_for_max(MG * (g + 1) + 8 * half + 2 * i + n)
                        if i % 2 and u >= 1:
                            weigh_values(u - 1, i // 2)
                        if half == 1 and i == 1 and g >= 1:
                            turn_out(g - 1)
                    if half == 1 and g + 1 < NG:
                        turn_max(g + 1)
                weigh_values(2 * NG - 1, 0)
                weigh_values(2 * NG - 1, 1)
                turn_out(NG - 1)
                wait("att_out", NG)
                turn(1)
                wait("xT_h", 2 * ND)
                wait("xT_l", 2 * ND)
                for i in range(NT):
                    split_product(bank[i][:, 0:D], lambda a, k: xT[a][:, k, P * i:P * (i + 1)],
                                  lambda c, k: woT[c][:, k, :], ND).then_inc(S["proj_sum"], 1)
                wait("xn_made", 2 * NT)
                turn(2)
                for n, to in enumerate((6, 7, 0, 1)):
                    for i in range(2):
                        last = pe.matmul(bank[to][:, D * i:D * (i + 1)], select[:, 2 * n + i, :], xn[:, 0, :],
                                         start=True, stop=True)
                    last.then_inc(S["bcast"], 1)
                wait("xT_h", 3 * ND)
                wait("xT_l", 3 * ND)
                wait("odd_made", ND)

                def up(k):
                    if k % 2 == 0:
                        wait("w1_h", k // 2 + 1)
                        wait("w1_l", k // 2 + 1)
                    if k >= 4:
                        wait("gelu_made", k - 3)
                    split_product(bank[2 + k % 4], lambda a, j: w1_now[a][:, j, P * k:P * (k + 1)],
                                  lambda c, j: xT[c][:, j, :], ND).then_inc(S["hid_sum"], 1)

                AHEAD = 3
                for k in range(AHEAD):
                    up(k)
                wait("w2_h", ND)
                wait("w2_l", ND)
                for k in range(NH):
                    wait("hid_h", k + 1)
                    wait("hid_l", k + 1)
                    for i in range(NT):
                        for n, (a, c) in enumerate(((0, 0), (0, 1), (1, 0))):
                            last = pe.matmul(bank[(0, 1, 6, 7)[i]][:, 0:D],
                                             hidT[a][:, k % RING, P * i:P * (i + 1)], w2_now[c][:, k, :],
                                             start=(k == 0 and n == 0), stop=(k == NH - 1 and n == 2))
                    last.then_inc(S["hid_used"], 1)
                    if k + AHEAD < NH:
                        up(k + AHEAD)
                wait("out_made", NT)


def _layouts(x, tok_v, tok_Wk, tok_Wq, tok_Wv, qkv_w, qkv_b, out_w, out_b, W1, b1, W2, b2, scale):
    idx = np.asarray(x)
    qkv_w, qkv_b = np.asarray(qkv_w), np.asarray(qkv_b)
    order = [part * D + (g * GH + hd) * HD + d
             for part in range(2) for g in range(NG) for d in range(HD) for hd in range(GH)]
    rows = np.concatenate([qkv_w[order], qkv_w[2 * D:]])
    return {
        "idx": idx.reshape(-1),
        "idx_cols": idx.reshape(B, NT, P)[:, :, ::-1].transpose(2, 0, 1).reshape(P, B * NT),
        "v_pad": np.concatenate([np.zeros(P - 1, np.float32), np.asarray(tok_v)[:, 0]]),
        "wq": np.asarray(tok_Wq), "wk": np.asarray(tok_Wk), "wvT": np.asarray(tok_Wv).T,
        "wqkvT": rows.T,
        "qk_bias": qkv_b[order].reshape(4, P).T, "v_bias": qkv_b[2 * D:],
        "woT": np.asarray(out_w).T, "out_bias": np.asarray(out_b),
        "w1T": np.asarray(W1).T, "b1_col": np.asarray(b1).reshape(NH, P).T,
        "w2T": np.asarray(W2).T, "b2": np.asarray(b2), "scale": np.asarray(scale).reshape(1),
    }


def kernel(**inputs):
    import concourse.bacc as _bacc
    from concourse.bass_utils import run_bass_kernel_spmd as _run

    names = ["x", "L0_tok_v", "L0_tok_Wk", "L0_tok_Wq", "L0_tok_Wv", "L0_attn_qkv_w", "L0_attn_qkv_b",
             "L0_attn_out_w", "L0_attn_out_b", "L0_ffn_W1", "L0_ffn_b1", "L0_ffn_W2", "L0_ffn_b2", "L0_ffn_scale"]
    laid = _layouts(*(inputs[n] for n in names))
    nc = _bacc.Bacc("TRN2", target_bir_lowering=False, num_devices=1)
    arrays, A = {}, {}
    for name, a in laid.items():
        a = np.ascontiguousarray(a)
        arrays[f"in_{name}_dram"] = a
        A[name] = nc.dram_tensor(f"in_{name}_dram", a.shape, mybir.dt.from_np(a.dtype), kind="ExternalInput").ap()
    A["out"] = nc.dram_tensor("out_dram", (B, T, D), F32, kind="ExternalOutput").ap()
    tower_kernel(nc, A)
    r = _run(nc, [arrays], core_ids=[0])
    return r.results[0]["out_dram"]
```

```python
from contextlib import ExitStack
from itertools import islice

import numpy as np
import concourse.bass as bass
from concourse import mybir

F32 = mybir.dt.float32
F32R = mybir.dt.float32r
I32 = mybir.dt.int32
ALU = mybir.AluOpType
ACT = mybir.ActivationFunctionType
AX = mybir.AxisListType

P = 128
B, T = 4, 512
D = 256
HID = 1024
HEADS, HD = 16, 16
NT = T // P
ND = D // P
NH = HID // P
GH = 4
NG = HEADS // GH
GR = GH * HD
VW = 32
MAXROW = 96
STK = MAXROW + 2
SLOTS = 3
LEAD = 24
EPS = 1e-5
RING = 3


def tower_kernel(nc, A):
    ctx = ExitStack()
    with ctx:
        def sb(name, shape, dt=F32):
            return ctx.enter_context(nc.sbuf_tensor(name, shape, dt))

        def sem(name):
            return ctx.enter_context(nc.semaphore(name))

        ident = sb("ident", [P, P])
        causal = sb("causal", [P, P])
        iota_free = sb("iota_free", [P, D])
        row_id = sb("row_id", [P, ND])
        minus_half = sb("minus_half", [P, NT])
        toep = [sb(f"toep_{c}", [P, T], F32R) for c in "hl"]
        g_mat = [sb(f"g_mat_{c}", [P, ND, D], F32R) for c in "hl"]
        wvT = [sb(f"wvT_{c}", [P, ND, D], F32R) for c in "hl"]
        wqkvT = [sb(f"wqkvT_{c}", [P, ND, 3 * D], F32R) for c in "hl"]
        woT = [sb(f"woT_{c}", [P, ND, D], F32R) for c in "hl"]
        qk_bias = sb("qk_bias", [P, 4])
        v_bias = sb("v_bias", [P, D])
        out_bias = sb("out_bias", [P, D])
        b1_col = sb("b1_col", [P, NH])
        b2_row = sb("b2_row", [P, D])
        scale = sb("scale", [P, 1])
        idx_row = sb("idx_row", [P, (B + 1) * T], I32)
        idx_col_i = sb("idx_col_i", [P, (B + 1) * NT], I32)
        idx_col = sb("idx_col", [P, (B + 1) * NT])

        onehot = sb("onehot", [P, NT, D], F32R)
        onehotT = sb("onehotT", [P, ND, T], F32R)
        pool_a = sb("pool_a", [P, 8704], F32R)
        h = sb("h", [P, NT, D])
        xn = sb("xn", [P, NT, D])
        xT = [sb(f"xT_{c}", [P, ND, T], F32R) for c in "hl"]
        stats = sb("stats", [P, NT, 6])
        mean_var = sb("mean_var", [P, NT, 2])
        var_eps = sb("var_eps", [P, NT])
        rstd = sb("rstd", [P, NT])
        k_stack = sb("k_stack", [P, SLOTS, GH * T], F32R)
        q_stack = sb("q_stack", [P, SLOTS, GH * T], F32R)
        v_ext = sb("v_ext", [P, NT, HEADS, VW])
        probs = sb("probs", [P, 8192])
        row_max = sb("row_max", [P, 2, GH * NT])
        neg_max = [sb(f"neg_max_{c}", [GH * NT, 2, P], F32R) for c in "hl"]
        attT = sb("attT", [P, T])
        inv_sum = sb("inv_sum", [P, NT, GH])
        odd_scaled = sb("odd_scaled", [P, ND, 8])
        hidT = [sb(f"hidT_{c}", [P, RING, T], F32R) for c in "hl"]

        def cut(at, *shape):
            n = int(np.prod(shape))
            names = " ".join(f"d{i}" for i in range(len(shape)))
            sizes = {f"d{i}": s for i, s in enumerate(shape[1:], 1)}
            v = pool_a[:, at:at + n]
            return v if len(shape) == 1 else v.rearrange(f"p ({names}) -> p {names}", **sizes)

        mixT = [cut(0, ND, T), cut(1024, ND, T)]
        qgT = [cut(2048, ND, T), cut(3072, ND, T)]
        ev = cut(4096, NT, 2, D)
        tri = [k * T - P * (k * (k - 1) // 2) for k in range(NT)]
        att = [cut(6144, 1280), cut(6144 + 1280, 1280)]
        qk = [cut(0, 4, T), cut(2048, 4, T)]
        w1_now = [cut(0, ND, HID), cut(2048, ND, HID)]
        w2_now = [cut(4096, NH, D), cut(6144, NH, D)]

        probs_ring = probs[:, :].rearrange("p (u h m n) -> p u h m n", u=2, h=GH, m=2)
        w1_full = probs[:, 0:2048].rearrange("p (j n) -> p j n", j=ND)
        w2_full = probs[:, 2048:4096].rearrange("p (k n) -> p k n", k=NH)
        gelu = probs[:, 4096:8192].rearrange("p (k n) -> p k n", k=NH)
        wstage = probs[:, :]

        def pb(name, shape):
            return ctx.enter_context(nc.psum_tensor(name, shape, F32))

        pair = [pb("pair0", [P, 2, T]), pb("pair1", [P, 2, T])]
        duo = pb("duo", [P, 2, T])
        solo = [pb("solo0", [P, T]), pb("solo1", [P, T])]
        bank = [pair[0][:, 0, :], pair[0][:, 1, :], pair[1][:, 0, :], pair[1][:, 1, :],
                duo[:, 0, :], duo[:, 1, :], solo[0][:, :], solo[1][:, :]]

        QG, MIX, EV, ATT = (2, 3, 4, 5), (0, 1), (6, 7, 2, 3), (4, 5, 0, 1)
        TOK, TURN, QK, V = (6, 7, 2, 3), ((4, 5), (4, 5), (2, 3)), (0, 1, 6, 7), (2, 3)
        SUM, UP = (0, 1, 6, 7), (2, 3, 4, 5)

        def max_bank(n):
            return (4, 5, 0, 1, 2, 3)[n % 6] if n < LEAD else 4 + n % 2

        loaded = sem("loaded")
        small_loaded = sem("small_loaded")
        w_loaded = [sem(f"w_loaded{i}") for i in range(4)]
        consts = sem("consts")
        split_h, split_l = sem("split_h"), sem("split_l")
        g_made, g_split_h = sem("g_made"), sem("g_split_h")
        v_set, stacks_set = sem("v_set"), sem("stacks_set")
        idx_ready = sem("idx_ready")
        S = {n: sem(n) for n in (
            "onehot_made", "qg_sum", "mix_sum", "ev_sum", "qg_h", "qg_l", "mix_h", "mix_l", "ev_act", "ev_dve",
            "att_sum", "att_masked", "att_h", "att_l", "tok_sum", "h_made",
            "eps_added", "rstd_made", "xn_made", "turned", "xT_h", "xT_l", "odd_made",
            "qk_sum", "qk_h", "qk_l", "v_sum", "v_made",
            "scores", "reduced", "max_turned", "max_h", "max_l",
            "scoresT", "exped", "pv_done", "attT_made", "att_turned", "recip", "att_out",
            "bias_added", "proj_sum", "resid", "b2_added", "bcast",
            "w1_made", "w1_h", "w1_l", "w2_made", "w2_h", "w2_l",
            "hid_sum", "gelu_made", "hid_h", "hid_l", "hid_used", "out_made")}
        stack_in = [sem(f"stack_in{g}") for g in range(NG)]
        max_in = [sem(f"max_in{g}") for g in range(NG)]
        ffn_in = sem("ffn_in")
        h_free = sem("h_free")

        def seq_waits(eng, b, count):
            def wait(name, k):
                eng.wait_ge(S[name], b * count[name] + k)
            return wait

        COUNT = dict(
            onehot_made=6, qg_sum=4, mix_sum=2, ev_sum=4, qg_h=2, qg_l=2, mix_h=2, mix_l=2, ev_act=2, ev_dve=2,
            att_sum=4, att_masked=4, att_h=4, att_l=4, tok_sum=4, h_made=4,
            eps_added=2, rstd_made=2, xn_made=8, turned=6, xT_h=6, xT_l=6, odd_made=2,
            qk_sum=4, qk_h=4, qk_l=4, v_sum=2, v_made=4,
            scores=64, reduced=64, max_turned=4, max_h=4, max_l=4,
            scoresT=32, exped=32, pv_done=8, attT_made=4, att_turned=4, recip=4, att_out=4,
            bias_added=4, proj_sum=4, resid=4, b2_added=4, bcast=4,
            w1_made=4, w1_h=4, w1_l=4, w2_made=2, w2_h=2, w2_l=2,
            hid_sum=8, gelu_made=8, hid_h=8, hid_l=8, hid_used=8, out_made=4)

        def f32(ap):
            return ap.bitcast(F32)

        SPLITS = [(toep, 0, T, 0), (wvT, T, ND * D, 0), (wqkvT, 1024, ND * 3 * D, 1), (woT, 2560, ND * D, 1)]

        def flat(t):
            v = t[:]
            return v if len(v.shape) == 2 else v.rearrange("p a b -> p (a b)")

        block = ctx.enter_context(nc.Block())

        @block.sync
        def _(sp):
            sp.dma_start(wstage[:, 3072:3584].rearrange("p (k n) -> p k n", k=ND),
                         A["wq"].rearrange("(k p) n -> p k n", p=P)).then_inc(w_loaded[2], 16)
            sp.dma_start(wstage[:, 3584:4096].rearrange("p (k n) -> p k n", k=ND),
                         A["wk"].rearrange("(k p) n -> p k n", p=P)).then_inc(w_loaded[2], 16)
            sp.dma_start(wstage[:, 0:T], bass.AP(A["v_pad"].tensor, 0, [[1, P], [1, T]])).then_inc(w_loaded[0], 16)
            sp.dma_start(wstage[:, T:1024].rearrange("p (k n) -> p k n", k=ND),
                         A["wvT"].rearrange("(k p) n -> p k n", p=P)).then_inc(w_loaded[0], 16)
            sp.dma_start(idx_col_i[:, 0:B * NT], A["idx_cols"]).then_inc(loaded, 16)
            sp.dma_start(idx_col_i[:, B * NT:], A["idx_cols"][:, 0:NT]).then_inc(loaded, 16)
            sp.dma_start(idx_row[:, 0:B * T], A["idx"].partition_broadcast(P)).then_inc(loaded, 16)
            sp.dma_start(idx_row[:, B * T:], A["idx"][0:T].partition_broadcast(P)).then_inc(loaded, 16)
            sp.dma_start(wstage[:, 1024:2560].rearrange("p (k n) -> p k n", k=ND),
                         A["wqkvT"].rearrange("(k p) n -> p k n", p=P)).then_inc(w_loaded[1], 16)
            sp.dma_start(wstage[:, 2560:3072].rearrange("p (k n) -> p k n", k=ND),
                         A["woT"].rearrange("(k p) n -> p k n", p=P)).then_inc(w_loaded[1], 16)
            sp.dma_start(qk_bias[:, :], A["qk_bias"]).then_inc(small_loaded, 16)
            sp.dma_start(v_bias[:, :], A["v_bias"].partition_broadcast(P)).then_inc(small_loaded, 16)
            sp.dma_start(out_bias[:, :], A["out_bias"].partition_broadcast(P)).then_inc(small_loaded, 16)
            sp.dma_start(b1_col[:, :], A["b1_col"]).then_inc(small_loaded, 16)
            sp.dma_start(b2_row[:, :], A["b2"].partition_broadcast(P)).then_inc(small_loaded, 16)
            sp.dma_start(scale[:, :], A["scale"].partition_broadcast(P)).then_inc(small_loaded, 16)
            sp.sem_inc(h_free, 1)
            sp.wait_ge(stacks_set, 2)
            with sp.Fori(0, B) as b:
                wait = seq_waits(sp, b, COUNT)

                def stack(g):
                    fb, at = g // 2, GR * (g % 2)
                    for dst, f, parts in ((k_stack, 2 + fb, (0, 1, 0)), (q_stack, fb, (0, 0, 1))):
                        for slot, part in enumerate(parts):
                            sp.dma_start(f32(dst[HD * slot:HD * (slot + 1), g % SLOTS, :]),
                                         f32(qk[part][at:at + GR, f, :])).then_inc(stack_in[g], 16)

                def stack_max(g):
                    wait("max_h", g + 1)
                    wait("max_l", g + 1)
                    for part in range(2):
                        sp.dma_start(f32(q_stack[MAXROW + part:MAXROW + part + 1, g % SLOTS, :]),
                                     f32(neg_max[part][:, g % 2, :])).then_inc(max_in[g], 16)

                wait("qk_h", 2)
                wait("qk_l", 2)
                stack(0)
                stack(1)
                wait("qk_h", 4)
                wait("qk_l", 4)
                stack(2)
                stack_max(0)
                wait("scoresT", 8)
                stack(3)
                for g in range(1, NG):
                    stack_max(g)
                wait("pv_done", 2 * NG)
                sp.dma_start(w1_full, A["w1T"]).then_inc(ffn_in, 16)
                sp.dma_start(w2_full, A["w2T"]).then_inc(ffn_in, 16)
                for i in range(NT):
                    wait("out_made", NT + i + 1)
                    sp.dma_start(A["out"][b, P * i:P * (i + 1), :], h[:, i, :]).then_inc(h_free, 16)
            sp.wait_ge(h_free, 64 * B + 1)

        @block.gpsimd
        def _(pool):
            pool.memset(ident[:, :], 0.0).then_inc(consts, 1)
            pool.memset(causal[:, :], 1.0).then_inc(consts, 1)
            pool.memset(minus_half[:, :], -0.5).then_inc(consts, 1)
            pool.iota(iota_free[:, :], [[1, D]], base=0, channel_multiplier=0,
                      allow_small_or_imprecise_dtypes=True).then_inc(consts, 1)
            pool.iota(row_id[:, :], [[P, ND]], base=0, channel_multiplier=1,
                      allow_small_or_imprecise_dtypes=True).then_inc(consts, 1)
            pool.wait_ge(consts, 5)
            pool.affine_select(out=ident[:, :], in_=ident[:, :], compare_op=ALU.not_equal, fill=1.0,
                               base=0, pattern=[[-1, P]], channel_multiplier=1).then_inc(consts, 1)
            pool.affine_select(out=causal[:, :], in_=causal[:, :], compare_op=ALU.is_ge, fill=0.0,
                               base=0, pattern=[[1, P]], channel_multiplier=-1).then_inc(consts, 1)
            for n, (dst, at, width, load) in enumerate(SPLITS):
                pool.wait_ge(w_loaded[load], 32)
                pool.tensor_scalar(flat(dst[0]), wstage[:, at:at + width], 1.0, 0.0, ALU.mult, ALU.add)\
                    .then_inc(split_h, 1)
            pool.memset(v_ext[:, :, :, HD:VW], 0.0).then_inc(v_set, 1)
            pool.wait_ge(v_set, 1)
            pool.memset(v_ext[:, :, :, HD:HD + 1], 1.0).then_inc(v_set, 1)
            pool.memset(f32(q_stack[0:MAXROW, :, :]), 0.0).then_inc(stacks_set, 1)
            pool.memset(f32(k_stack[0:STK, :, :]), 1.0).then_inc(stacks_set, 1)
            pool.wait_ge(small_loaded, 16 * 6)
            with pool.Fori(0, B) as b:
                wait = seq_waits(pool, b, COUNT)

                def inverse_std(n):
                    wait("eps_added", n + 1)
                    pool.tensor_tensor(rstd[:, :], var_eps[:, :], minus_half[:, :], ALU.pow)\
                        .then_inc(S["rstd_made"], 1)

                inverse_std(0)
                wait("xn_made", NT)
                for i in range(NT):
                    pool.tensor_tensor(h[:, i, :], h[:, i, :], out_bias[:, :], ALU.add)\
                        .then_inc(S["bias_added"], 1)
                inverse_std(1)
                wait("xn_made", 2 * NT)
                for i in range(NT):
                    pool.tensor_tensor(h[:, i, :], h[:, i, :], b2_row[:, :], ALU.add)\
                        .then_inc(S["b2_added"], 1)

        @block.scalar
        def _(act):
            for j in range(ND):
                act.wait_ge(g_made, j + 1)
                act.activation(g_mat[0][:, j, :], bank[j][:, 0:D], ACT.Copy).then_inc(g_split_h, 1)
            act.wait_ge(small_loaded, 16 * 6)
            with act.Fori(0, B) as b:
                wait = seq_waits(act, b, COUNT)

                def turned_high(n):
                    for j in range(ND):
                        wait("turned", ND * n + j + 1)
                        act.activation(xT[0][:, j, :], bank[TURN[n][j]], ACT.Copy).then_inc(S["xT_h"], 1)

                for j in range(ND):
                    wait("qg_sum", 2 * j + 1)
                    act.activation(qgT[0][:, j, :], bank[QG[2 * j]], ACT.Copy).then_inc(S["qg_h"], 1)
                for j in range(ND):
                    wait("mix_sum", j + 1)
                    act.activation(mixT[0][:, j, :], bank[MIX[j]], ACT.Copy).then_inc(S["mix_h"], 1)
                for n, i in enumerate((0, 2)):
                    wait("ev_sum", i + 1)
                    act.activation(ev[:, i, :, :], bank[EV[i]], ACT.Copy).then_inc(S["ev_act"], 1)
                for k in range(NT):
                    wait("att_masked", k + 1)
                    act.activation(att[0][:, tri[k]:tri[k] + T - P * k], bank[ATT[k]][:, P * k:T], ACT.Copy)\
                        .then_inc(S["att_h"], 1)
                act.wait_ge(h_free, b * 64 + 1)
                for i in range(NT):
                    wait("tok_sum", i + 1)
                    act.activation(h[:, i, :], bank[TOK[i]][:, 0:D], ACT.Copy, bias=0.001)\
                        .then_inc(S["h_made"], 1)
                turned_high(0)
                for n, f in enumerate((2, 0, 3, 1)):
                    wait("qk_sum", n + 1)
                    act.activation(qk[0][:, f, :], bank[QK[n]], ACT.Identity, bias=qk_bias[:, f:f + 1])\
                        .then_inc(S["qk_h"], 1)

                def max_high(g):
                    wait("max_turned", g + 1)
                    act.activation(neg_max[0][:, g % 2, :], bank[7][0:GH * NT, 0:P], ACT.Copy, scale=-1.0)\
                        .then_inc(S["max_h"], 1)

                max_high(0)
                for g in range(NG):
                    for half in range(2):
                        u = 2 * g + half
                        for i in range(GH):
                            n = GH * u + i
                            wait("scoresT", n + 1)
                            if u >= 2 and i == 0:
                                wait("pv_done", u - 1)
                            act.activation(probs_ring[:, u % 2, i, :, :], pair[n % 2][:, :, :], ACT.Exp,
                                           scale=float(HD) ** -0.5).then_inc(S["exped"], 1)
                            if half == 1 and i == 0 and g + 1 < NG:
                                max_high(g + 1)
                            if half == 0 and i == 3 and g >= 1:
                                wait("pv_done", 2 * g)
                                act.activation(attT[:, :], bank[6], ACT.Copy).then_inc(S["attT_made"], 1)
                wait("pv_done", 2 * NG)
                act.activation(attT[:, :], bank[6], ACT.Copy).then_inc(S["attT_made"], 1)
                turned_high(1)
                turned_high(2)
                for i in range(4):
                    wait("w1_made", i + 1)
                    cols = slice(D * i, D * (i + 1))
                    act.activation(w1_now[0][:, :, cols], w1_full[:, :, cols], ACT.Copy).then_inc(S["w1_h"], 1)
                for j in range(ND):
                    wait("w2_made", j + 1)
                    act.activation(w2_now[0][:, j::ND, :], w2_full[:, j::ND, :], ACT.Copy).then_inc(S["w2_h"], 1)

                def hidden_high(k):
                    if k >= RING:
                        wait("hid_used", k - RING + 1)
                    act.wait_ge(S["gelu_made"], b * NH + k + 1)
                    act.activation(hidT[0][:, k % RING, :], gelu[:, k, :], ACT.Copy).then_inc(S["hid_h"], 1)

                for k in range(NH):
                    wait("hid_sum", k + 1)
                    act.activation(gelu[:, k, :], bank[UP[k % 4]], ACT.Gelu, bias=b1_col[:, k:k + 1])\
                        .then_inc(S["gelu_made"], 1)
                    if k:
                        hidden_high(k - 1)
                hidden_high(NH - 1)

        @block.vector
        def _(dve):
            def one_hot(step, seq):
                if step < ND:
                    dve.tensor_scalar(onehotT[:, step, :], idx_row[:, bass.ds(seq * T, T)],
                                      row_id[:, step:step + 1], None, ALU.is_equal).then_inc(S["onehot_made"], 1)
                else:
                    i = step - ND
                    dve.tensor_scalar(onehot[:, i, :], iota_free[:, :], idx_col[:, bass.ds(seq * NT + i, 1)], None,
                                      ALU.is_equal).then_inc(S["onehot_made"], 1)

            dve.wait_ge(loaded, 16 * 4)
            dve.tensor_copy(idx_col[:, :], idx_col_i[:, :]).then_inc(idx_ready, 1)
            dve.wait_ge(consts, 7)
            dve.wait_ge(idx_ready, 1)
            for step in range(6):
                one_hot(step, 0)
            dve.sem_inc(S["out_made"], NT)
            def weight_low(n):
                dst, at, width, _ = SPLITS[n]
                dve.wait_ge(split_h, n + 1)
                dve.tensor_tensor(flat(dst[1]), wstage[:, at:at + width], f32(flat(dst[0])), ALU.subtract)\
                    .then_inc(split_l, 1)

            for j in range(ND):
                dve.wait_ge(g_split_h, j + 1)
                dve.tensor_tensor(g_mat[1][:, j, :], bank[j][:, 0:D], f32(g_mat[0][:, j, :]), ALU.subtract)\
                    .then_inc(split_l, 1)
            for n in range(len(SPLITS)):
                weight_low(n)
            dve.wait_ge(small_loaded, 16 * 6)
            with dve.Fori(0, B) as b:
                wait = seq_waits(dve, b, COUNT)

                def norm(n):
                    for i in range(NT):
                        wait("resid" if n else "h_made", i + 1)
                        dve.bn_stats(stats[:, i, :], h[:, i, :])
                    dve.drain()
                    for i in range(NT):
                        dve.bn_aggr(mean_var[:, i, :], stats[:, i, :])
                    dve.drain()
                    dve.tensor_scalar(var_eps[:, :], mean_var[:, :, 1], EPS, None, ALU.add)\
                        .then_inc(S["eps_added"], 1)
                    wait("rstd_made", n + 1)
                    for i in range(NT):
                        dve.tensor_scalar(xn[:, i, :], h[:, i, :], mean_var[:, i, 0:1], rstd[:, i:i + 1],
                                          ALU.subtract, ALU.mult).then_inc(S["xn_made"], 1)

                def turned_low(n):
                    for j in range(ND):
                        wait("xT_h", ND * n + j + 1)
                        dve.tensor_tensor(xT[1][:, j, :], bank[TURN[n][j]], f32(xT[0][:, j, :]),
                                          ALU.subtract).then_inc(S["xT_l"], 1)

                for j in range(ND):
                    wait("qg_sum", 2 * j + 2)
                    dve.tensor_copy(qgT[1][:, j, :], bank[QG[2 * j + 1]]).then_inc(S["qg_l"], 1)
                for j in range(ND):
                    wait("mix_h", j + 1)
                    dve.tensor_tensor(mixT[1][:, j, :], bank[MIX[j]], f32(mixT[0][:, j, :]), ALU.subtract)\
                        .then_inc(S["mix_l"], 1)
                for n, i in enumerate((1, 3)):
                    wait("ev_sum", i + 1)
                    dve.tensor_copy(ev[:, i, :, :], bank[EV[i]]).then_inc(S["ev_dve"], 1)

                def att_low(k):
                    wait("att_h", k + 1)
                    cols = slice(tri[k], tri[k] + T - P * k)
                    dve.tensor_tensor(att[1][:, cols], bank[ATT[k]][:, P * k:T], f32(att[0][:, cols]),
                                      ALU.subtract).then_inc(S["att_l"], 1)

                for k in range(NT):
                    wait("att_sum", k + 1)
                    diag = bank[ATT[k]][:, P * k:P * (k + 1)]
                    dve.tensor_tensor(diag, diag, causal[:, :], ALU.mult).then_inc(S["att_masked"], 1)
                    if k:
                        att_low(k - 1)
                att_low(NT - 1)
                norm(0)
                turned_low(0)
                for n, f in enumerate((2, 0, 3, 1)):
                    wait("qk_h", n + 1)
                    dve.scalar_tensor_tensor(out=qk[1][:, f, :], in0=bank[QK[n]],
                                             scalar=qk_bias[:, f:f + 1], in1=f32(qk[0][:, f, :]),
                                             op0=ALU.add, op1=ALU.subtract).then_inc(S["qk_l"], 1)
                    if n != 1:
                        continue
                    for i in range(NT):
                        wait("v_sum", i // 2 + 1)
                        dve.tensor_tensor(
                            v_ext[:, i, :, 0:HD],
                            bank[V[i // 2]][:, D * (i % 2):D * (i % 2 + 1)].rearrange("p (h d) -> p h d", d=HD),
                            v_bias[:, :].rearrange("p (h d) -> p h d", d=HD), ALU.add).then_inc(S["v_made"], 1)

                def max_of(n):
                    g = n // (GH * NT)
                    at = n % (GH * NT)
                    wait("scores", n + 1)
                    dve.reduce_max(row_max[:, g % 2, at:at + 1], bank[max_bank(n)], axis=AX.X)\
                        .then_inc(S["reduced"], 1)

                def max_low(g):
                    wait("max_h", g + 1)
                    dve.scalar_tensor_tensor(out=neg_max[1][:, g % 2, :], in0=bank[7][0:GH * NT, 0:P], scalar=-1.0,
                                             in1=f32(neg_max[0][:, g % 2, :]), op0=ALU.mult, op1=ALU.subtract)\
                        .then_inc(S["max_l"], 1)

                def normalise(g):
                    wait("att_turned", g + 1)
                    o = bank[7].rearrange("p (n h w) -> p n h w", n=NT, h=GH)
                    dve.reciprocal(inv_sum[:, :, :], o[:, :, :, HD]).then_inc(S["recip"], 1)
                    wait("recip", g + 1)
                    dve.tensor_tensor(
                        xn[:, :, GR * g:GR * (g + 1)].rearrange("p n (h d) -> p n h d", h=GH), o[:, :, :, 0:HD],
                        inv_sum[:, :, :].unsqueeze(3).broadcast_to([P, NT, GH, HD]), ALU.mult)\
                        .then_inc(S["att_out"], 1)

                def w1_low(i):
                    wait("w1_h", i + 1)
                    cols = slice(D * i, D * (i + 1))
                    dve.tensor_tensor(w1_now[1][:, :, cols], w1_full[:, :, cols], f32(w1_now[0][:, :, cols]),
                                      ALU.subtract).then_inc(S["w1_l"], 1)

                MG = GH * NT
                for n in range(NG * MG):
                    max_of(n)
                    if n % MG == 1 and n > MG:
                        max_low(n // MG - 1)
                    if n == LEAD + 31:
                        normalise(0)
                max_low(NG - 1)
                for g in range(1, NG - 1):
                    normalise(g)
                normalise(NG - 1)
                turned_low(1)
                for i in range(NT):
                    wait("bias_added", i + 1)
                    wait("proj_sum", i + 1)
                    dve.tensor_tensor(h[:, i, :], bank[i][:, 0:D], h[:, i, :], ALU.add).then_inc(S["resid"], 1)
                norm(1)
                turned_low(2)
                for j in range(ND):
                    dve.tensor_scalar(odd_scaled[:, j, :], bank[2 + j][:, 2:18:2], scale[:, 0:1], None, ALU.mult)\
                        .then_inc(S["odd_made"], 1)
                wait("odd_made", ND)
                dve.wait_ge(ffn_in, b * 32 + 32)
                for i in range(4):
                    wait("bcast", i // 2 + 1)
                    for j in range(ND):
                        last = dve.scalar_tensor_tensor(
                            out=w1_full[:, j, D * i:D * (i + 1)], in0=bank[6 + i // 2][:, D * (i % 2):D * (i % 2 + 1)],
                            scalar=odd_scaled[:, j, i:i + 1], in1=w1_full[:, j, D * i:D * (i + 1)],
                            op0=ALU.mult, op1=ALU.add)
                    last.then_inc(S["w1_made"], 1)
                    if i:
                        w1_low(i - 1)
                w1_low(3)
                for j in range(ND):
                    for i in range(4):
                        wait("bcast", 2 + i // 2 + 1)
                        last = dve.scalar_tensor_tensor(
                            out=w2_full[:, j::ND, 64 * i:64 * (i + 1)],
                            in0=bank[i // 2][:, D * (i % 2):D * (i % 2 + 1)].rearrange("p (q r) -> p r q", r=4),
                            scalar=odd_scaled[:, j, 4 + i:5 + i], in1=w2_full[:, j::ND, 64 * i:64 * (i + 1)],
                            op0=ALU.mult, op1=ALU.add)
                    last.then_inc(S["w2_made"], 1)
                for j in range(ND):
                    wait("w2_h", j + 1)
                    dve.tensor_tensor(w2_now[1][:, j::ND, :], w2_full[:, j::ND, :], f32(w2_now[0][:, j::ND, :]),
                                      ALU.subtract).then_inc(S["w2_l"], 1)
                for k in range(NH):
                    if k >= 2:
                        one_hot(k - 2, b + 1)
                    wait("hid_h", k + 1)
                    if k >= RING:
                        wait("hid_used", k - RING + 1)
                    dve.tensor_tensor(hidT[1][:, k % RING, :], gelu[:, k, :], f32(hidT[0][:, k % RING, :]),
                                      ALU.subtract).then_inc(S["hid_l"], 1)
                for i in range(NT):
                    wait("b2_added", i + 1)
                    wait("hid_used", NH)
                    dve.tensor_tensor(h[:, i, :], bank[SUM[i]][:, 0:D], h[:, i, :], ALU.add)\
                        .then_inc(S["out_made"], 1)

        @block.tensor
        def _(pe):
            def split_product(out, lhs, rhs, inner):
                passes = [(k, a, c) for k in range(inner) for a, c in ((0, 0), (0, 1), (1, 0))]
                for n, (k, a, c) in enumerate(passes):
                    last = pe.matmul(out, lhs(a, k), rhs(c, k), start=(n == 0), stop=(n == len(passes) - 1))
                return last

            wq = wstage[:, 3072:3584].rearrange("p (k n) -> p k n", k=ND)
            wk = wstage[:, 3584:4096].rearrange("p (k n) -> p k n", k=ND)
            pe.wait_ge(w_loaded[2], 32)
            for j in range(ND):
                for k in range(ND):
                    last = pe.matmul(bank[j][:, 0:D], wq[:, k, P * j:P * (j + 1)], wk[:, k, :],
                                     start=(k == 0), stop=(k == ND - 1))
                last.then_inc(g_made, 1)
            pe.wait_ge(split_l, ND + 2)
            pe.wait_ge(consts, 7)
            with pe.Fori(0, B) as b:
                wait = seq_waits(pe, b, COUNT)
                wait("onehot_made", 2)
                for j in range(ND):
                    for part in range(2):
                        for k in range(ND):
                            last = pe.matmul(bank[QG[2 * j + part]], g_mat[part][:, k, P * j:P * (j + 1)],
                                             onehotT[:, k, :], start=(k == 0), stop=(k == ND - 1))
                        last.then_inc(S["qg_sum"], 1)
                wait("onehot_made", 6)
                pe.wait_ge(S["out_made"], b * NT + NT)
                for j in range(ND):
                    for part in range(2):
                        for k in range(NT):
                            last = pe.matmul(bank[MIX[j]][:, P * k:T], onehot[:, k, P * j:P * (j + 1)],
                                             toep[part][:, 0:T - P * k], start=(part == 0 and k == 0),
                                             stop=(part == 1 and k == NT - 1))
                    last.then_inc(S["mix_sum"], 1)
                for i in range(NT):
                    if i == 2:
                        wait("qg_h", 1)
                    if i == 3:
                        wait("qg_l", 1)
                    for part in range(2):
                        for k in range(ND):
                            last = pe.matmul(bank[EV[i]][:, D * part:D * (part + 1)],
                                             onehotT[:, k, P * i:P * (i + 1)], wvT[part][:, k, :],
                                             start=(k == 0), stop=(k == ND - 1))
                    last.then_inc(S["ev_sum"], 1)
                wait("qg_h", 2)
                wait("qg_l", 2)
                wait("mix_h", 2)
                wait("mix_l", 2)
                for k in range(NT):
                    split_product(bank[ATT[k]][:, P * k:T], lambda a, j: mixT[a][:, j, P * k:P * (k + 1)],
                                  lambda c, j: qgT[c][:, j, P * k:T], ND).then_inc(S["att_sum"], 1)
                wait("ev_act", 2)
                wait("ev_dve", 2)
                for i in range(NT):
                    wait("att_h", i + 1)
                    wait("att_l", i + 1)
                    split_product(bank[TOK[i]][:, 0:D],
                                  lambda a, k: att[a][:, tri[k] + P * (i - k):tri[k] + P * (i - k + 1)],
                                  lambda c, k: ev[:, k, c, :], i + 1).then_inc(S["tok_sum"], 1)

                def turn(n):
                    for j in range(ND):
                        for i in range(NT):
                            last = pe.transpose(bank[TURN[n][j]][:, P * i:P * (i + 1)],
                                                xn[:, i, P * j:P * (j + 1)], ident[:, :])
                        last.then_inc(S["turned"], 1)
                    
                wait("xn_made", NT)
                turn(0)
                pe.wait_ge(split_l, ND + len(SPLITS))
                pe.wait_ge(v_set, 2)
                wait("xT_h", ND)
                wait("xT_l", ND)
                for n, f in enumerate((2, 0, 3, 1)):
                    split_product(bank[QK[n]], lambda a, k: wqkvT[a][:, k, P * f:P * (f + 1)],
                                  lambda c, k: xT[c][:, k, :], ND).then_inc(S["qk_sum"], 1)
                    if n == 1:
                        for i in range(NT):
                            last = split_product(bank[V[i // 2]][:, D * (i % 2):D * (i % 2 + 1)],
                                                 lambda a, k: xT[a][:, k, P * i:P * (i + 1)],
                                                 lambda c, k: wqkvT[c][:, k, 2 * D:3 * D], ND)
                            if i % 2:
                                last.then_inc(S["v_sum"], 1)

                def scores_for_max(n):
                    g, hd, i = n // (GH * NT), n // NT % GH, n % NT
                    if n == 0:
                        wait("qk_l", 2)
                    elif n == 4:
                        wait("v_made", NT)
                    elif n >= 6:
                        wait("reduced", n - 5 if n < LEAD else n - 1)
                    if n % (GH * NT) == 0:
                        pe.wait_ge(stack_in[g], b * 96 + 96)
                    at = T * hd
                    pe.matmul(bank[max_bank(n)], q_stack[0:80, g % SLOTS, at + P * i:at + P * (i + 1)],
                              k_stack[0:80, g % SLOTS, at:at + T], start=True, stop=True).then_inc(S["scores"], 1)

                def turn_max(g):
                    wait("reduced", GH * NT * (g + 1))
                    if g == 0:
                        wait("qk_h", 4)
                        wait("qk_l", 4)
                    elif g < 3:
                        wait("max_l", g)
                    else:
                        wait("att_out", g - 2)
                    pe.transpose(bank[7][0:GH * NT, 0:P], row_max[:, g % 2, :], ident[:, :])\
                        .then_inc(S["max_turned"], 1)

                def scoresT_pair(u, i):
                    g, half, n = u // 2, u % 2, GH * u + i
                    if half == 0 and i == 0:
                        pe.wait_ge(max_in[g], b * 32 + 32)
                    if n >= 2:
                        wait("exped", n - 1)
                    else:
                        wait("reduced", LEAD)
                    for m in range(2):
                        at = T * i + P * (2 * half + m)
                        last = pe.matmul(pair[n % 2][:, m, :], k_stack[0:STK, g % SLOTS, at:at + P],
                                         q_stack[0:STK, g % SLOTS, T * i:T * (i + 1)], start=True, stop=True)
                    last.then_inc(S["scoresT"], 1)

                def weigh_values(u, m):
                    g, half = u // 2, u % 2
                    if m == 0:
                        wait("exped", GH * (u + 1))
                        if half == 0 and g >= 1:
                            wait("attT_made", g)
                    for i in range(GH):
                        last = pe.matmul(bank[6][VW * i:VW * (i + 1), :], v_ext[:, 2 * half + m, GH * g + i, :],
                                         probs_ring[:, u % 2, i, m, :], start=(half == 0 and m == 0),
                                         stop=(half == 1 and m == 1))
                    if m == 1:
                        last.then_inc(S["pv_done"], 1)

                def turn_out(g):
                    wait("attT_made", g + 1)
                    if g < 2:
                        wait("max_l", g + 3)
                    else:
                        wait("att_out", g)
                    for i in range(NT):
                        last = pe.transpose(bank[7][:, P * i:P * (i + 1)], attT[:, P * i:P * (i + 1)], ident[:, :])
                    last.then_inc(S["att_turned"], 1)

                MG = GH * NT
                for n in range(LEAD):
                    scores_for_max(n)
                    if n == MG + 1:
                        turn_max(0)
                left = iter(range(LEAD, NG * MG))

                def more_scores(count):
                    for n in islice(left, count):
                        scores_for_max(n)

                for u in range(2 * NG):
                    g, half = u // 2, u % 2
                    for i in range(GH):
                        scoresT_pair(u, i)
                        more_scores(1)
                        if half == 1 and i == 0 and g + 1 < NG:
                            turn_max(g + 1)
                        if i % 2:
                            if u >= 1:
                                weigh_values(u - 1, i // 2)
                            more_scores(2)
                    if half == 1 and g >= 1:
                        turn_out(g - 1)
                weigh_values(2 * NG - 1, 0)
                weigh_values(2 * NG - 1, 1)
                turn_out(NG - 1)
                wait("att_out", NG)
                turn(1)
                wait("xT_h", 2 * ND)
                wait("xT_l", 2 * ND)
                for i in range(NT):
                    split_product(bank[i][:, 0:D], lambda a, k: xT[a][:, k, P * i:P * (i + 1)],
                                  lambda c, k: woT[c][:, k, :], ND).then_inc(S["proj_sum"], 1)
                wait("xn_made", 2 * NT)
                turn(2)
                for n, to in enumerate((6, 7, 0, 1)):
                    for i in range(2):
                        token = 2 * (2 * n + i) + 1
                        last = pe.matmul(bank[to][:, D * i:D * (i + 1)], ident[:, token:token + 1].broadcast_to([P, P]), xn[:, 0, :],
                                         start=True, stop=True)
                    last.then_inc(S["bcast"], 1)
                wait("xT_h", 3 * ND)
                wait("xT_l", 3 * ND)
                wait("odd_made", ND)

                def up(k):
                    if k % 2 == 0:
                        wait("w1_h", k // 2 + 1)
                        wait("w1_l", k // 2 + 1)
                    if k >= 4:
                        wait("gelu_made", k - 3)
                    split_product(bank[UP[k % 4]], lambda a, j: w1_now[a][:, j, P * k:P * (k + 1)],
                                  lambda c, j: xT[c][:, j, :], ND).then_inc(S["hid_sum"], 1)

                AHEAD = 3
                for k in range(AHEAD):
                    up(k)
                wait("w2_h", ND)
                wait("w2_l", ND)
                for k in range(NH):
                    wait("hid_h", k + 1)
                    wait("hid_l", k + 1)
                    for i in range(NT):
                        for n, (a, c) in enumerate(((0, 0), (0, 1), (1, 0))):
                            last = pe.matmul(bank[SUM[i]][:, 0:D],
                                             hidT[a][:, k % RING, P * i:P * (i + 1)], w2_now[c][:, k, :],
                                             start=(k == 0 and n == 0), stop=(k == NH - 1 and n == 2))
                    last.then_inc(S["hid_used"], 1)
                    if k + AHEAD < NH:
                        up(k + AHEAD)


def _layouts(x, tok_v, tok_Wk, tok_Wq, tok_Wv, qkv_w, qkv_b, out_w, out_b, W1, b1, W2, b2, scale):
    idx = np.asarray(x)
    qkv_w, qkv_b = np.asarray(qkv_w), np.asarray(qkv_b)
    order = [part * D + (g * GH + hd) * HD + d
             for part in range(2) for g in range(NG) for d in range(HD) for hd in range(GH)]
    rows = np.concatenate([qkv_w[order], qkv_w[2 * D:]])
    return {
        "idx": idx.reshape(-1),
        "idx_cols": idx.reshape(B, NT, P)[:, :, ::-1].transpose(2, 0, 1).reshape(P, B * NT),
        "v_pad": np.concatenate([np.zeros(P - 1, np.float32), np.asarray(tok_v)[:, 0]]),
        "wq": np.asarray(tok_Wq), "wk": np.asarray(tok_Wk), "wvT": np.asarray(tok_Wv).T,
        "wqkvT": rows.T,
        "qk_bias": qkv_b[order].reshape(4, P).T, "v_bias": qkv_b[2 * D:],
        "woT": np.asarray(out_w).T, "out_bias": np.asarray(out_b),
        "w1T": np.asarray(W1).T.reshape(ND, P, HID).transpose(1, 0, 2), "b1_col": np.asarray(b1).reshape(NH, P).T,
        "w2T": np.asarray(W2).T.reshape(NH, P, D).transpose(1, 0, 2), "b2": np.asarray(b2), "scale": np.asarray(scale).reshape(1),
    }


def kernel(**inputs):
    import concourse.bacc as _bacc
    from concourse.bass_utils import run_bass_kernel_spmd as _run

    names = ["x", "L0_tok_v", "L0_tok_Wk", "L0_tok_Wq", "L0_tok_Wv", "L0_attn_qkv_w", "L0_attn_qkv_b",
             "L0_attn_out_w", "L0_attn_out_b", "L0_ffn_W1", "L0_ffn_b1", "L0_ffn_W2", "L0_ffn_b2", "L0_ffn_scale"]
    laid = _layouts(*(inputs[n] for n in names))
    nc = _bacc.Bacc("TRN2", target_bir_lowering=False, num_devices=1)
    arrays, A = {}, {}
    for name, a in laid.items():
        a = np.ascontiguousarray(a)
        arrays[f"in_{name}_dram"] = a
        A[name] = nc.dram_tensor(f"in_{name}_dram", a.shape, mybir.dt.from_np(a.dtype), kind="ExternalInput").ap()
    A["out"] = nc.dram_tensor("out_dram", (B, T, D), F32, kind="ExternalOutput").ap()
    tower_kernel(nc, A)
    r = _run(nc, [arrays], core_ids=[0])
    return r.results[0]["out_dram"]
```

```python
from contextlib import ExitStack
from itertools import islice

import numpy as np
import concourse.bass as bass
from concourse import mybir

F32 = mybir.dt.float32
F32R = mybir.dt.float32r
I32 = mybir.dt.int32
ALU = mybir.AluOpType
ACT = mybir.ActivationFunctionType
AX = mybir.AxisListType

P = 128
B, T = 4, 512
D = 256
HID = 1024
HEADS, HD = 16, 16
NT = T // P
ND = D // P
NH = HID // P
GH = 4
NG = HEADS // GH
GR = GH * HD
VW = 32
MAXROW = 96
STK = MAXROW + 2
SLOTS = 3
MG = GH * NT
LEAD = MG + 8
EARLY = 5
STEPS = NG * NT
ATT_STEP = 10
NARROW = 11
WIDE = GH * NARROW
LAST = STEPS - 2
GELUS = 4
EPS = 1e-5
PROBS = 3
RING = 2


def tower_kernel(nc, A):
    ctx = ExitStack()
    with ctx:
        def sb(name, shape, dt=F32):
            return ctx.enter_context(nc.sbuf_tensor(name, shape, dt))

        def sem(name):
            return ctx.enter_context(nc.semaphore(name))

        one_r = sb("one_r", [P, P], F32R)
        ident = one_r[:, :].bitcast(F32)
        causal = sb("causal", [P, P])
        iota_free = sb("iota_free", [P, D])
        row_id = sb("row_id", [P, ND])
        minus_half = sb("minus_half", [P, NT])
        toep = [sb(f"toep_{c}", [P, T], F32R) for c in "hl"]
        g_mat = [sb(f"g_mat_{c}", [P, ND, D], F32R) for c in "hl"]
        wvT = [sb(f"wvT_{c}", [P, ND, D], F32R) for c in "hl"]
        wqkvT = [sb(f"wqkvT_{c}", [P, ND, 3 * D], F32R) for c in "hl"]
        woT = [sb(f"woT_{c}", [P, ND, D], F32R) for c in "hl"]
        qk_bias = sb("qk_bias", [P, 4])
        v_bias = sb("v_bias", [P, D])
        out_bias = sb("out_bias", [P, D])
        b1_col = sb("b1_col", [P, NH])
        b2_row = sb("b2_row", [P, D])
        scale = sb("scale", [P, 1])
        idx_row = sb("idx_row", [P, T], I32)
        idx_col_i = sb("idx_col_i", [P, (B + 1) * NT], I32)
        idx_col = sb("idx_col", [P, (B + 1) * NT])

        onehot = sb("onehot", [P, NT, D], F32R)
        onehotT = sb("onehotT", [P, ND, T], F32R)
        pool_a = sb("pool_a", [P, 8192], F32R)
        tok = sb("tok", [P, NT, D])
        tok_n = sb("tok_n", [P, NT, D])
        qk = [sb(f"qk_{c}", [P, 4, T], F32R) for c in "hl"]
        h = sb("h", [P, NT, D])
        xn = sb("xn", [P, NT, D])
        xT = [sb(f"xT_{c}", [P, ND, T], F32R) for c in "hl"]
        stats = sb("stats", [P, NT, 6])
        mean_var = sb("mean_var", [P, NT, 2])
        var_eps = sb("var_eps", [P, NT])
        rstd = sb("rstd", [P, NT])
        shift = sb("shift", [P, NT])
        table_switch = sb("table_switch", [P, 1])
        k_stack = sb("k_stack", [P, SLOTS, GH * T], F32R)
        q_stack = sb("q_stack", [P, SLOTS, GH * T], F32R)
        v_ext = sb("v_ext", [P, NT, HEADS, VW])
        probs = sb("probs", [P, PROBS * GH * T])
        row_max = sb("row_max", [P, 2, MG])
        neg_max = [sb(f"neg_max_{c}", [MG, 2, P], F32R) for c in "hl"]
        attT = sb("attT", [P, T])
        inv_sum = sb("inv_sum", [P, NT, GH])
        odd_scaled = sb("odd_scaled", [P, ND, 8])
        hidT = [sb(f"hidT_{c}", [P, RING, T], F32R) for c in "hl"]

        def cut(pool, at, *shape):
            n = int(np.prod(shape))
            names = " ".join(f"d{i}" for i in range(len(shape)))
            sizes = {f"d{i}": s for i, s in enumerate(shape[1:], 1)}
            v = pool[:, at:at + n]
            return v if len(shape) == 1 else v.rearrange(f"p ({names}) -> p {names}", **sizes)

        mixT = xT
        qgT = [hidT[c][:, 0:ND, :] for c in range(2)]
        ev = cut(pool_a, 2560, NT, 2, D)
        tri = [k * T - P * (k * (k - 1) // 2) for k in range(NT)]
        att = [cut(pool_a, 0, 1280), cut(pool_a, 1280, 1280)]
        w1_now = [cut(pool_a, 0, ND, HID), cut(pool_a, 2048, ND, HID)]
        w2_now = [cut(pool_a, 4096, NH, D), cut(pool_a, 6144, NH, D)]

        probs_ring = probs[:, :].rearrange("p (s h n) -> p s h n", s=PROBS, h=GH)
        w1_full = probs[:, 2048:4096].rearrange("p (j n) -> p j n", j=ND)
        w2_full = probs[:, 4096:6144].rearrange("p (k n) -> p k n", k=NH)
        gelu = probs[:, 0:2048].rearrange("p (k n) -> p k n", k=GELUS)
        ident_made = attT[:, 0:P]
        rows = [hidT[c][:, 0, 0:D] for c in range(2)]
        wstage = probs[:, :]

        def pb(name, shape):
            return ctx.enter_context(nc.psum_tensor(name, shape, F32))

        bank = [pb(f"bank{n}", [P, T])[:, :] for n in range(8)]

        QG, EV, MIX = (0, 1, 2, 3), (0, 1, 2, 3), (0, 1)
        ATT_FIRST, TOK_FIRST = (2, 3, 0, 1), (2, 3, 0, 1)
        ATT, TOK = (4,) * NT, (7, 5, 6, 4)
        TOK_ORDER = (2, 3, 0, 1)
        TURN, QK, V = ((2, 3), (4, 5), (2, 3)), (4, 5, 2, 3), (2, 3)
        ODD, SUM, UP = 4, (0, 1, 6, 7), (2, 3, 4, 5)

        def max_bank(n):
            return (4 if n < LEAD else 3) + n % 3

        def scoresT_bank(n):
            return n % 3 if n < WIDE else (2, 0, 1, 3, 5)[(n - WIDE) % 5]

        idx_in = sem("idx_in")
        cols_in = sem("cols_in")
        small_loaded = sem("small_loaded")
        w_loaded = [sem(f"w_loaded{i}") for i in range(4)]
        consts = sem("consts")
        split_h, split_l = sem("split_h"), sem("split_l")
        g_made, g_split_h = sem("g_made"), sem("g_split_h")
        v_set, stacks_set = sem("v_set"), sem("stacks_set")
        idx_ready = sem("idx_ready")
        S = {n: sem(n) for n in (
            "onehot_made", "qg_sum", "mix_sum", "ev_sum", "qg_made", "mix_h", "mix_l", "ev_made",
            "att_sum", "att_masked", "att_h", "att_l", "tok_sum", "tok_made",
            "tok_eps", "tok_rstd", "tok_normed", "h_eps", "h_rstd", "h_normed", "h_shift", "rest_normed",
            "turned", "xT_h", "xT_l", "rows_h", "rows_l", "odd_turned", "odd_made",
            "qk_sum", "qk_h", "qk_l", "v_sum", "v_made",
            "scores", "reduced", "max_turned", "max_h", "max_l",
            "scoresT", "exped", "pv_done", "attT_made", "att_turned", "recip", "att_out",
            "bias_added", "proj_sum", "resid", "b2_added", "bcast",
            "w1_made", "w1_h", "w1_l", "w2_made", "w2_h", "w2_l",
            "hid_sum", "gelu_made", "hid_h", "hid_l", "hid_used", "out_made")}
        stack_in = [sem(f"stack_in{g}") for g in range(NG)]
        max_in = [sem(f"max_in{g}") for g in range(NG)]
        w1_in, w2_in = sem("w1_in"), sem("w2_in")
        h_free = sem("h_free")

        def seq_waits(eng, b, ahead=0):
            def wait(name, k):
                eng.wait_ge(S[name], b * COUNT[name] + (ahead * COUNT[name] + k))
            return wait

        COUNT = dict(
            onehot_made=6, qg_sum=4, mix_sum=2, ev_sum=4, qg_made=4, mix_h=2, mix_l=2, ev_made=4,
            att_sum=4, att_masked=4, att_h=4, att_l=4, tok_sum=4, tok_made=4,
            tok_eps=1, tok_rstd=1, tok_normed=4, h_eps=2, h_rstd=2, h_normed=1, h_shift=1, rest_normed=3,
            turned=6, xT_h=6, xT_l=6, rows_h=1, rows_l=1, odd_turned=1, odd_made=1,
            qk_sum=4, qk_h=4, qk_l=4, v_sum=2, v_made=4,
            scores=64, reduced=64, max_turned=4, max_h=4, max_l=4,
            scoresT=64, exped=64, pv_done=16, attT_made=4, att_turned=4, recip=4, att_out=4,
            bias_added=4, proj_sum=4, resid=4, b2_added=4, bcast=4,
            w1_made=4, w1_h=4, w1_l=4, w2_made=2, w2_h=2, w2_l=2,
            hid_sum=8, gelu_made=8, hid_h=8, hid_l=8, hid_used=8, out_made=4)

        def f32(ap):
            return ap.bitcast(F32)

        SPLITS = [(toep, 0, T, 0), (wvT, T, ND * D, 0), (wqkvT, 1024, ND * 3 * D, 1), (woT, 2560, ND * D, 1)]

        def flat(t):
            v = t[:]
            return v if len(v.shape) == 2 else v.rearrange("p a b -> p (a b)")

        block = ctx.enter_context(nc.Block())

        @block.sync
        def _(sp):
            sp.dma_start(idx_row[:, :], A["idx"][0].partition_broadcast(P)).then_inc(idx_in, 16)
            sp.dma_start(idx_col_i[:, :], A["idx_cols"]).then_inc(cols_in, 16)
            sp.dma_start(wstage[:, 3072:3584].rearrange("p (k n) -> p k n", k=ND),
                         A["wq"].rearrange("(k p) n -> p k n", p=P)).then_inc(w_loaded[2], 16)
            sp.dma_start(wstage[:, 3584:4096].rearrange("p (k n) -> p k n", k=ND),
                         A["wk"].rearrange("(k p) n -> p k n", p=P)).then_inc(w_loaded[2], 16)
            sp.dma_start(wstage[:, 0:T], bass.AP(A["v_pad"].tensor, 0, [[1, P], [1, T]])).then_inc(w_loaded[0], 16)
            sp.dma_start(wstage[:, T:1024].rearrange("p (k n) -> p k n", k=ND),
                         A["wvT"].rearrange("(k p) n -> p k n", p=P)).then_inc(w_loaded[0], 16)
            sp.dma_start(wstage[:, 1024:2560].rearrange("p (k n) -> p k n", k=ND),
                         A["wqkvT"].rearrange("(k p) n -> p k n", p=P)).then_inc(w_loaded[1], 16)
            sp.dma_start(wstage[:, 2560:3072].rearrange("p (k n) -> p k n", k=ND),
                         A["woT"].rearrange("(k p) n -> p k n", p=P)).then_inc(w_loaded[1], 16)
            sp.dma_start(qk_bias[:, :], A["qk_bias"]).then_inc(small_loaded, 16)
            sp.dma_start(v_bias[:, :], A["v_bias"].partition_broadcast(P)).then_inc(small_loaded, 16)
            sp.dma_start(out_bias[:, :], A["out_bias"].partition_broadcast(P)).then_inc(small_loaded, 16)
            sp.dma_start(b1_col[:, :], A["b1_col"]).then_inc(small_loaded, 16)
            sp.dma_start(b2_row[:, :], A["b2"].partition_broadcast(P)).then_inc(small_loaded, 16)
            sp.dma_start(scale[:, :], A["scale"].partition_broadcast(P)).then_inc(small_loaded, 16)
            sp.sem_inc(h_free, 1)
            sp.wait_ge(S["onehot_made"], ND)
            sp.dma_start(idx_row[:, :], A["idx"][1].partition_broadcast(P)).then_inc(idx_in, 16)
            sp.wait_ge(stacks_set, 2)

            def k_rows(g):
                for slot, part in enumerate((0, 1, 0)):
                    sp.dma_start(f32(k_stack[HD * slot:HD * (slot + 1), g % SLOTS, :]),
                                 f32(qk[part][GR * (g % 2):GR * (g % 2 + 1), 2 + g // 2, :])).then_inc(stack_in[g], 16)

            def q_rows(g):
                for slot, part in enumerate((0, 0, 1)):
                    sp.dma_start(f32(q_stack[HD * slot:HD * (slot + 1), g % SLOTS, :]),
                                 f32(qk[part][GR * (g % 2):GR * (g % 2 + 1), g // 2, :])).then_inc(stack_in[g], 16)

            def first_stacks(wait):
                wait("qk_h", 1)
                wait("qk_l", 1)
                k_rows(0)
                wait("qk_h", 2)
                wait("qk_l", 2)
                q_rows(0)
                k_rows(1)
                q_rows(1)

            first_stacks(seq_waits(sp, 0))

            def sequence(b, more):
                wait = seq_waits(sp, b)

                def stack_max(g):
                    wait("max_h", g + 1)
                    wait("max_l", g + 1)
                    for part in range(2):
                        sp.dma_start(f32(q_stack[MAXROW + part:MAXROW + part + 1, g % SLOTS, :]),
                                     f32(neg_max[part][:, g % 2, :])).then_inc(max_in[g], 16)

                if more:
                    seq_waits(sp, b, 1)("onehot_made", ND)
                    sp.dma_start(idx_row[:, :], A["idx"][b + 2].partition_broadcast(P)).then_inc(idx_in, 16)
                wait("qk_h", 4)
                wait("qk_l", 4)
                k_rows(2)
                q_rows(2)
                stack_max(0)
                stack_max(1)
                wait("scoresT", MG)
                k_rows(3)
                q_rows(3)
                stack_max(2)
                stack_max(3)
                wait("pv_done", STEPS - PROBS + 1)
                sp.dma_start(w1_full, A["w1T"]).then_inc(w1_in, 16)
                wait("pv_done", STEPS - PROBS + 2)
                sp.dma_start(w2_full, A["w2T"]).then_inc(w2_in, 16)
                if more:
                    first_stacks(seq_waits(sp, b, 1))
                for i in range(NT):
                    wait("out_made", i + 1)
                    sp.dma_start(A["out"][b, P * i:P * (i + 1), :], h[:, i, :]).then_inc(h_free, 16)

            with sp.Fori(0, B - 1) as b:
                sequence(b, True)
            sequence(B - 1, False)
            sp.wait_ge(h_free, 64 * B + 1)

        @block.gpsimd
        def _(pool):
            pool.memset(ident_made, 0.0).then_inc(consts, 1)
            pool.memset(causal[:, :], 1.0).then_inc(consts, 1)
            pool.memset(minus_half[:, :], -0.5).then_inc(consts, 1)
            pool.iota(iota_free[:, :], [[1, D]], base=0, channel_multiplier=0,
                      allow_small_or_imprecise_dtypes=True).then_inc(consts, 1)
            pool.iota(row_id[:, :], [[P, ND]], base=0, channel_multiplier=1,
                      allow_small_or_imprecise_dtypes=True).then_inc(consts, 1)
            pool.wait_ge(consts, 5)
            pool.affine_select(out=ident_made, in_=ident_made, compare_op=ALU.not_equal, fill=1.0,
                               base=0, pattern=[[-1, P]], channel_multiplier=1).then_inc(consts, 1)
            pool.affine_select(out=causal[:, :], in_=causal[:, :], compare_op=ALU.is_ge, fill=0.0,
                               base=0, pattern=[[1, P]], channel_multiplier=-1).then_inc(consts, 1)
            pool.wait_ge(consts, 6)
            pool.tensor_scalar(one_r[:, :], ident_made, 1.0, 0.0, ALU.mult, ALU.add).then_inc(consts, 1)
            for n, (dst, at, width, load) in enumerate(SPLITS):
                pool.wait_ge(w_loaded[load], 32)
                pool.tensor_scalar(flat(dst[0]), wstage[:, at:at + width], 1.0, 0.0, ALU.mult, ALU.add)\
                    .then_inc(split_h, 1)
            pool.memset(v_ext[:, :, :, HD:VW], 0.0).then_inc(v_set, 1)
            pool.wait_ge(v_set, 1)
            pool.memset(v_ext[:, :, :, HD:HD + 1], 1.0).then_inc(v_set, 1)
            pool.memset(f32(q_stack[0:MAXROW, :, :]), 0.0).then_inc(stacks_set, 1)
            pool.memset(f32(k_stack[0:STK, :, :]), 1.0).then_inc(stacks_set, 1)
            pool.wait_ge(small_loaded, 16 * 6)

            def inverse_std(wait, norm, part, first, last):
                wait(f"{norm}_eps", part + 1)
                pool.tensor_tensor(rstd[:, first:last], var_eps[:, first:last], minus_half[:, first:last], ALU.pow)\
                    .then_inc(S[f"{norm}_rstd"], 1)

            inverse_std(seq_waits(pool, 0), "tok", 0, 0, NT)

            def sequence(b, more):
                wait = seq_waits(pool, b)
                pool.wait_ge(h_free, b * 64 + 1)
                for i in range(NT):
                    wait("tok_made", i + 1)
                    pool.tensor_tensor(h[:, i, :], tok[:, i, :], out_bias[:, :], ALU.add)\
                        .then_inc(S["bias_added"], 1)
                inverse_std(wait, "h", 0, 0, 1)
                inverse_std(wait, "h", 1, 1, NT)
                for i in range(4):
                    wait("w1_h", i + 1)
                    cols = slice(D * i, D * (i + 1))
                    pool.tensor_tensor(w1_now[1][:, :, cols], w1_full[:, :, cols], f32(w1_now[0][:, :, cols]),
                                       ALU.subtract).then_inc(S["w1_l"], 1)
                if more:
                    inverse_std(seq_waits(pool, b, 1), "tok", 0, 0, NT)
                wait("h_normed", 1)
                wait("rest_normed", NT - 1)
                for i in range(NT):
                    pool.tensor_tensor(h[:, i, :], h[:, i, :], b2_row[:, :], ALU.add)\
                        .then_inc(S["b2_added"], 1)

            with pool.Fori(0, B - 1) as b:
                sequence(b, True)
            sequence(B - 1, False)

        @block.scalar
        def _(act):
            for j in range(ND):
                act.wait_ge(g_made, j + 1)
                act.activation(g_mat[0][:, j, :], bank[j][:, 0:D], ACT.Copy).then_inc(g_split_h, 1)

            def tok_operands(wait):
                for j in range(ND):
                    for part in range(2):
                        wait("qg_sum", 2 * j + part + 1)
                        act.activation(qgT[part][:, j, :], bank[QG[2 * j + part]], ACT.Copy).then_inc(S["qg_made"], 1)
                for i in range(NT):
                    wait("ev_sum", i + 1)
                    act.activation(ev[:, i, :, :], bank[EV[i]], ACT.Copy).then_inc(S["ev_made"], 1)

            def mix_high(wait, j):
                wait("mix_sum", j + 1)
                act.activation(mixT[0][:, j, :], bank[MIX[j]], ACT.Copy).then_inc(S["mix_h"], 1)

            def tok_out(wait, n, i, banks):
                wait("tok_sum", n + 1)
                act.activation(tok[:, i, :], bank[banks[i]][:, 0:D], ACT.Copy, bias=0.001)\
                    .then_inc(S["tok_made"], 1)

            def turned_high(wait, n, j):
                wait("turned", ND * n + j + 1)
                act.activation(xT[0][:, j, :], bank[TURN[n][j]], ACT.Copy).then_inc(S["xT_h"], 1)

            def qk_high(wait, n):
                f = (2, 0, 3, 1)[n]
                wait("qk_sum", n + 1)
                act.activation(qk[0][:, f, :], bank[QK[n]], ACT.Identity, bias=qk_bias[:, f:f + 1])\
                    .then_inc(S["qk_h"], 1)

            first = seq_waits(act, 0)
            tok_operands(first)
            for j in range(ND):
                mix_high(first, j)
            for i in range(NT):
                tok_out(first, i, i, TOK_FIRST)
            for j in range(ND):
                turned_high(first, 0, j)
            act.wait_ge(small_loaded, 16 * 6)
            for n in range(4):
                qk_high(first, n)

            def sequence(b, more):
                wait, wait_next = seq_waits(act, b), seq_waits(act, b, 1)

                def max_high(g):
                    wait("max_turned", g + 1)
                    act.activation(neg_max[0][:, g % 2, :], bank[7][0:MG, 0:P], ACT.Copy, scale=-1.0)\
                        .then_inc(S["max_h"], 1)

                if more:
                    tok_operands(wait_next)
                max_high(0)
                if more:
                    for j in range(ND):
                        mix_high(wait_next, j)
                for s in range(STEPS):
                    g, kb = s // NT, s % NT
                    for i in range(GH):
                        n = GH * s + i
                        wait("scoresT", n + 1)
                        if s >= PROBS and i == 0:
                            wait("pv_done", s - PROBS + 1)
                        act.activation(probs_ring[:, s % PROBS, i, :], bank[scoresT_bank(n)], ACT.Exp,
                                       scale=float(HD) ** -0.5).then_inc(S["exped"], 1)
                        if i == 1 and kb == 2 and g + 1 < NG:
                            max_high(g + 1)
                        if i == 0 and kb == 1 and g >= 1:
                            wait("pv_done", NT * g)
                            act.activation(attT[:, :], bank[6], ACT.Copy).then_inc(S["attT_made"], 1)
                turned_high(wait, 1, 0)
                wait("pv_done", STEPS)
                act.activation(attT[:, :], bank[6], ACT.Copy).then_inc(S["attT_made"], 1)
                act.activation(table_switch[:, 0:1], minus_half[:, 0:1], ACT.Gelu)
                turned_high(wait, 1, 1)
                if more:
                    wait("bias_added", NT)
                    for n, i in enumerate(TOK_ORDER):
                        tok_out(wait_next, n, i, TOK)
                wait("h_normed", 1)
                act.activation(rows[0], xn[:, 0, :], ACT.Copy).then_inc(S["rows_h"], 1)
                wait("h_rstd", 2)
                wait("h_shift", 1)
                for i in range(1, NT):
                    act.activation(xn[:, i, :], h[:, i, :], ACT.Identity, scale=rstd[:, i:i + 1],
                                   bias=shift[:, i:i + 1]).then_inc(S["rest_normed"], 1)
                for j in range(ND):
                    turned_high(wait, 2, j)

                def w1_high(i):
                    wait("w1_made", i + 1)
                    cols = slice(D * i, D * (i + 1))
                    act.activation(w1_now[0][:, :, cols], w1_full[:, :, cols], ACT.Copy).then_inc(S["w1_h"], 1)

                w1_high(0)
                w1_high(1)

                def w2_high(j):
                    wait("w2_made", j + 1)
                    act.activation(w2_now[0][:, j::ND, :], w2_full[:, j::ND, :], ACT.Copy).then_inc(S["w2_h"], 1)

                def hidden_high(k):
                    if k >= RING:
                        wait("hid_used", k - RING + 1)
                    act.wait_ge(S["gelu_made"], b * NH + k + 1)
                    act.activation(hidT[0][:, k % RING, :], gelu[:, k % GELUS, :], ACT.Copy).then_inc(S["hid_h"], 1)

                for k in range(NH):
                    wait("hid_sum", k + 1)
                    if k >= GELUS:
                        wait("hid_l", k - GELUS + 1)
                    act.activation(gelu[:, k % GELUS, :], bank[UP[k % 4]], ACT.Gelu, bias=b1_col[:, k:k + 1])\
                        .then_inc(S["gelu_made"], 1)
                    if more and k == NH - 1:
                        for j in range(ND):
                            turned_high(wait_next, 0, j)
                    if k:
                        hidden_high(k - 1)
                    if k < ND:
                        w2_high(k)
                        w1_high(2 + k)
                hidden_high(NH - 1)
                if more:
                    for n in range(4):
                        qk_high(wait_next, n)
                        if n == 1:
                            act.activation(table_switch[:, 0:1], minus_half[:, 0:1], ACT.Exp)

            with act.Fori(0, B - 1) as b:
                sequence(b, True)
            sequence(B - 1, False)

        @block.vector
        def _(dve):
            def one_hot(step, seq):
                if step < ND:
                    dve.tensor_scalar(onehotT[:, step, :], idx_row[:, :],
                                      row_id[:, step:step + 1], None, ALU.is_equal).then_inc(S["onehot_made"], 1)
                else:
                    i = step - ND
                    dve.tensor_scalar(onehot[:, i, :], iota_free[:, :], idx_col[:, bass.ds(seq * NT + i, 1)], None,
                                      ALU.is_equal).then_inc(S["onehot_made"], 1)

            dve.wait_ge(cols_in, 16)
            dve.tensor_copy(idx_col[:, :], idx_col_i[:, :]).then_inc(idx_ready, 1)
            dve.wait_ge(idx_in, 16)
            dve.wait_ge(consts, 8)
            dve.wait_ge(idx_ready, 1)
            for step in range(6):
                one_hot(step, 0)

            def weight_low(n):
                dst, at, width, _ = SPLITS[n]
                dve.wait_ge(split_h, n + 1)
                dve.tensor_tensor(flat(dst[1]), wstage[:, at:at + width], f32(flat(dst[0])), ALU.subtract)\
                    .then_inc(split_l, 1)

            for j in range(ND):
                dve.wait_ge(g_split_h, j + 1)
                dve.tensor_tensor(g_mat[1][:, j, :], bank[j][:, 0:D], f32(g_mat[0][:, j, :]), ALU.subtract)\
                    .then_inc(split_l, 1)
            for n in (0, 1):
                weight_low(n)

            def mix_low(wait, j):
                wait("mix_h", j + 1)
                dve.tensor_tensor(mixT[1][:, j, :], bank[MIX[j]], f32(mixT[0][:, j, :]), ALU.subtract)\
                    .then_inc(S["mix_l"], 1)

            def att_split(wait, k, banks):
                wait("att_sum", k + 1)
                diag = bank[banks[k]][:, P * k:P * (k + 1)]
                dve.tensor_tensor(diag, diag, causal[:, :], ALU.mult).then_inc(S["att_masked"], 1)
                cols = slice(tri[k], tri[k] + T - P * k)
                wait("att_masked", k + 1)
                dve.tensor_copy(att[0][:, cols], bank[banks[k]][:, P * k:T]).then_inc(S["att_h"], 1)
                wait("att_h", k + 1)
                dve.tensor_tensor(att[1][:, cols], bank[banks[k]][:, P * k:T], f32(att[0][:, cols]),
                                  ALU.subtract).then_inc(S["att_l"], 1)

            def row_stats(wait, src, made, i):
                wait(made, i + 1)
                dve.bn_stats(stats[:, i, :], src[:, i, :])

            def variance(norm, first, last):
                dve.drain()
                for i in range(first, last):
                    dve.bn_aggr(mean_var[:, i, :], stats[:, i, :])
                dve.drain()
                dve.tensor_scalar(var_eps[:, first:last], mean_var[:, first:last, 1], EPS, None, ALU.add)\
                    .then_inc(S[f"{norm}_eps"], 1)

            def apply_norm(wait, dst, src, norm, part, first, last):
                wait(f"{norm}_rstd", part + 1)
                for i in range(first, last):
                    dve.tensor_scalar(dst[:, i, :], src[:, i, :], mean_var[:, i, 0:1], rstd[:, i:i + 1],
                                      ALU.subtract, ALU.mult).then_inc(S[f"{norm}_normed"], 1)

            def turned_low(wait, n, j):
                wait("xT_h", ND * n + j + 1)
                dve.tensor_tensor(xT[1][:, j, :], bank[TURN[n][j]], f32(xT[0][:, j, :]),
                                  ALU.subtract).then_inc(S["xT_l"], 1)

            def qk_low(wait, n):
                f = (2, 0, 3, 1)[n]
                wait("qk_h", n + 1)
                dve.scalar_tensor_tensor(out=qk[1][:, f, :], in0=bank[QK[n]],
                                         scalar=qk_bias[:, f:f + 1], in1=f32(qk[0][:, f, :]),
                                         op0=ALU.add, op1=ALU.subtract).then_inc(S["qk_l"], 1)

            def values(wait, i):
                wait("v_sum", i // 2 + 1)
                dve.tensor_tensor(
                    v_ext[:, i, :, 0:HD],
                    bank[V[i // 2]][:, D * (i % 2):D * (i % 2 + 1)].rearrange("p (h d) -> p h d", d=HD),
                    v_bias[:, :].rearrange("p (h d) -> p h d", d=HD), ALU.add).then_inc(S["v_made"], 1)

            def max_of(wait, n):
                g = n // MG
                at = n % MG
                wait("scores", n + 1)
                dve.reduce_max(row_max[:, g % 2, at:at + 1], bank[max_bank(n)], axis=AX.X)\
                    .then_inc(S["reduced"], 1)

            def values_and_maxima(wait):
                for i in range(NT):
                    values(wait, i)
                for n in range(EARLY):
                    if n < 2:
                        qk_low(wait, 2 + n)
                    max_of(wait, n)

            first = seq_waits(dve, 0)
            for j in range(ND):
                mix_low(first, j)
            for k in range(NT):
                att_split(first, k, ATT_FIRST)
            for i in range(NT):
                row_stats(first, tok, "tok_made", i)
            variance("tok", 0, NT)
            weight_low(2)
            apply_norm(first, tok_n, tok, "tok", 0, 0, NT)
            for j in range(ND):
                turned_low(first, 0, j)
            dve.wait_ge(small_loaded, 16 * 6)
            dve.wait_ge(v_set, 1)
            for n in (0, 1):
                qk_low(first, n)
            dve.wait_ge(idx_in, 32)
            for step in range(6):
                one_hot(step, 1)
            weight_low(3)
            values_and_maxima(first)

            def sequence(b, more):
                wait, wait_next = seq_waits(dve, b), seq_waits(dve, b, 1)

                def max_low(g):
                    wait("max_h", g + 1)
                    dve.scalar_tensor_tensor(out=neg_max[1][:, g % 2, :], in0=bank[7][0:MG, 0:P], scalar=-1.0,
                                             in1=f32(neg_max[0][:, g % 2, :]), op0=ALU.mult, op1=ALU.subtract)\
                        .then_inc(S["max_l"], 1)

                def normalise(g):
                    wait("att_turned", g + 1)
                    o = bank[7].rearrange("p (n h w) -> p n h w", n=NT, h=GH)
                    dve.reciprocal(inv_sum[:, :, :], o[:, :, :, HD]).then_inc(S["recip"], 1)
                    wait("recip", g + 1)
                    dve.tensor_tensor(
                        xn[:, :, GR * g:GR * (g + 1)].rearrange("p n (h d) -> p n h d", h=GH), o[:, :, :, 0:HD],
                        inv_sum[:, :, :].unsqueeze(3).broadcast_to([P, NT, GH, HD]), ALU.mult)\
                        .then_inc(S["att_out"], 1)

                for n in range(EARLY, MG + 5):
                    max_of(wait, n)
                    if n == MG + 1:
                        max_low(0)
                    if more and n >= MG + 3:
                        mix_low(wait_next, n - MG - 3)
                for n in range(MG + 5, NG * MG):
                    max_of(wait, n)
                    if n % MG == 2 and n > 2 * MG:
                        max_low(n // MG - 1)
                    if n == 3 * MG - 1:
                        normalise(0)
                normalise(1)
                max_low(NG - 1)
                if more:
                    for k in range(NT):
                        att_split(wait_next, k, ATT)
                normalise(2)
                turned_low(wait, 1, 0)
                normalise(3)
                turned_low(wait, 1, 1)
                for i in range(NT):
                    wait("bias_added", i + 1)
                    wait("proj_sum", i + 1)
                    dve.tensor_tensor(h[:, i, :], bank[i][:, 0:D], h[:, i, :], ALU.add).then_inc(S["resid"], 1)
                    if i == 0:
                        row_stats(wait, h, "resid", 0)
                        variance("h", 0, 1)
                for i in range(1, NT):
                    row_stats(wait, h, "resid", i)
                variance("h", 1, NT)
                apply_norm(wait, xn, h, "h", 0, 0, 1)
                wait("rows_h", 1)
                dve.tensor_tensor(rows[1], xn[:, 0, :], f32(rows[0]), ALU.subtract).then_inc(S["rows_l"], 1)
                wait("odd_turned", 1)
                dve.tensor_scalar(odd_scaled[:, :, :], bank[ODD].rearrange("p (j n) -> p j n", n=P)[:, 0:ND, 2:18:2],
                                  scale[:, 0:1], None, ALU.mult).then_inc(S["odd_made"], 1)
                wait("h_rstd", 2)
                dve.scalar_tensor_tensor(out=shift[:, 1:NT], in0=mean_var[:, 1:NT, 0], scalar=-1.0, in1=rstd[:, 1:NT],
                                         op0=ALU.mult, op1=ALU.mult).then_inc(S["h_shift"], 1)
                wait("odd_made", 1)
                dve.wait_ge(w1_in, b * 16 + 16)

                def w1_fold(i):
                    wait("bcast", i // 2 + 1)
                    for j in range(ND):
                        last = dve.scalar_tensor_tensor(
                            out=w1_full[:, j, D * i:D * (i + 1)], in0=bank[6 + i // 2][:, D * (i % 2):D * (i % 2 + 1)],
                            scalar=odd_scaled[:, j, i:i + 1], in1=w1_full[:, j, D * i:D * (i + 1)],
                            op0=ALU.mult, op1=ALU.add)
                    last.then_inc(S["w1_made"], 1)

                def w2_fold(j):
                    for i in range(4):
                        wait("bcast", 2 + i // 2 + 1)
                        last = dve.scalar_tensor_tensor(
                            out=w2_full[:, j::ND, 64 * i:64 * (i + 1)],
                            in0=bank[i // 2][:, D * (i % 2):D * (i % 2 + 1)].rearrange("p (q r) -> p r q", r=4),
                            scalar=odd_scaled[:, j, 4 + i:5 + i], in1=w2_full[:, j::ND, 64 * i:64 * (i + 1)],
                            op0=ALU.mult, op1=ALU.add)
                    last.then_inc(S["w2_made"], 1)

                def w2_low(j):
                    wait("w2_h", j + 1)
                    dve.tensor_tensor(w2_now[1][:, j::ND, :], w2_full[:, j::ND, :], f32(w2_now[0][:, j::ND, :]),
                                      ALU.subtract).then_inc(S["w2_l"], 1)

                dve.wait_ge(w2_in, b * 16 + 16)
                w1_fold(0)
                for j in range(ND):
                    turned_low(wait, 2, j)
                w1_fold(1)
                w2_fold(0)
                w2_fold(1)
                w1_fold(2)
                w2_low(0)
                w1_fold(3)
                if more:
                    dve.wait_ge(idx_in, b * 16 + 48)
                for k in range(NH):
                    if k == 1:
                        w2_low(1)
                    if more and k == 3:
                        wait_next("tok_made", NT)
                        for i in range(NT):
                            dve.bn_stats(stats[:, i, :], tok[:, i, :])
                        variance("tok", 0, NT)
                    if more and k == 4:
                        apply_norm(wait_next, tok_n, tok, "tok", 0, 0, NT)
                    if more and k >= 5:
                        one_hot(2 * (k - 5), b + 2)
                        one_hot(2 * (k - 5) + 1, b + 2)
                    if more and k == NH - 2:
                        for j in range(ND):
                            turned_low(wait_next, 0, j)
                    wait("hid_h", k + 1)
                    if k >= RING:
                        wait("hid_used", k - RING + 1)
                    dve.tensor_tensor(hidT[1][:, k % RING, :], gelu[:, k % GELUS, :], f32(hidT[0][:, k % RING, :]),
                                      ALU.subtract).then_inc(S["hid_l"], 1)
                if more:
                    for n in (0, 1):
                        qk_low(wait_next, n)
                for i in range(NT):
                    wait("b2_added", i + 1)
                    wait("hid_used", NH)
                    dve.tensor_tensor(h[:, i, :], bank[SUM[i]][:, 0:D], h[:, i, :], ALU.add)\
                        .then_inc(S["out_made"], 1)
                if more:
                    values_and_maxima(wait_next)

            with dve.Fori(0, B - 1) as b:
                sequence(b, True)
            sequence(B - 1, False)

        @block.tensor
        def _(pe):
            def split_product(out, lhs, rhs, inner):
                passes = [(k, a, c) for k in range(inner) for a, c in ((0, 0), (0, 1), (1, 0))]
                for n, (k, a, c) in enumerate(passes):
                    last = pe.matmul(out, lhs(a, k), rhs(c, k), start=(n == 0), stop=(n == len(passes) - 1))
                return last

            wq = wstage[:, 3072:3584].rearrange("p (k n) -> p k n", k=ND)
            wk = wstage[:, 3584:4096].rearrange("p (k n) -> p k n", k=ND)
            pe.wait_ge(w_loaded[2], 32)
            for j in range(ND):
                for k in range(ND):
                    last = pe.matmul(bank[j][:, 0:D], wq[:, k, P * j:P * (j + 1)], wk[:, k, :],
                                     start=(k == 0), stop=(k == ND - 1))
                last.then_inc(g_made, 1)

            def qg_product(j, part):
                for k in range(ND):
                    last = pe.matmul(bank[QG[2 * j + part]], g_mat[part][:, k, P * j:P * (j + 1)],
                                     onehotT[:, k, :], start=(k == 0), stop=(k == ND - 1))
                last.then_inc(S["qg_sum"], 1)

            def mix_product(wait, j):
                wait("ev_made", j + 1)
                for part in range(2):
                    for k in range(NT):
                        last = pe.matmul(bank[MIX[j]][:, P * k:T], onehot[:, k, P * j:P * (j + 1)],
                                         toep[part][:, 0:T - P * k], start=(part == 0 and k == 0),
                                         stop=(part == 1 and k == NT - 1))
                last.then_inc(S["mix_sum"], 1)

            def ev_product(wait, i):
                wait("qg_made", i + 1)
                for part in range(2):
                    for k in range(ND):
                        last = pe.matmul(bank[EV[i]][:, D * part:D * (part + 1)],
                                         onehotT[:, k, P * i:P * (i + 1)], wvT[part][:, k, :],
                                         start=(k == 0), stop=(k == ND - 1))
                last.then_inc(S["ev_sum"], 1)

            def att_product(wait, k, banks):
                wait("mix_l", ND)
                split_product(bank[banks[k]][:, P * k:T], lambda a, j: mixT[a][:, j, P * k:P * (k + 1)],
                              lambda c, j: qgT[c][:, j, P * k:T], ND).then_inc(S["att_sum"], 1)

            def tok_product(wait, i, banks):
                wait("att_l", i + 1)
                split_product(bank[banks[i]][:, 0:D],
                              lambda a, k: att[a][:, tri[k] + P * (i - k):tri[k] + P * (i - k + 1)],
                              lambda c, k: ev[:, k, c, :], i + 1).then_inc(S["tok_sum"], 1)

            pe.wait_ge(split_l, ND + 2)
            pe.wait_ge(consts, 8)
            first = seq_waits(pe, 0)
            first("onehot_made", 6)
            for j in range(ND):
                for part in range(2):
                    qg_product(j, part)
            for i in range(NT):
                ev_product(first, i)
            for j in range(ND):
                mix_product(first, j)
            first("ev_made", NT)
            for k in range(NT):
                att_product(first, k, ATT_FIRST)
            for i in range(NT):
                tok_product(first, i, TOK_FIRST)

            def turn(n, src, j, wait_block=None):
                for i in range(NT):
                    if wait_block:
                        wait_block(i)
                    last = pe.transpose(bank[TURN[n][j]][:, P * i:P * (i + 1)],
                                        src[:, i, P * j:P * (j + 1)], ident[:, :])
                last.then_inc(S["turned"], 1)

            def value_products(half):
                for i in range(2 * half, 2 * half + 2):
                    last = split_product(bank[V[i // 2]][:, D * (i % 2):D * (i % 2 + 1)],
                                         lambda a, k: xT[a][:, k, P * i:P * (i + 1)],
                                         lambda c, k: wqkvT[c][:, k, 2 * D:3 * D], ND)
                    if i % 2:
                        last.then_inc(S["v_sum"], 1)

            def qk_product(wait, n):
                f = (2, 0, 3, 1)[n]
                if n >= 2:
                    wait("v_made", 2 * n - 2)
                split_product(bank[QK[n]], lambda a, k: wqkvT[a][:, k, P * f:P * (f + 1)],
                              lambda c, k: xT[c][:, k, :], ND).then_inc(S["qk_sum"], 1)

            def scores_for_max(b, ahead, n):
                g, hd, i = n // MG, n // NT % GH, n % NT
                if n >= 3:
                    seq_waits(pe, b, ahead)("reduced", n - 2)
                if n % MG == 0:
                    pe.wait_ge(stack_in[g], b * 96 + (ahead * 96 + 96))
                at = T * hd
                pe.matmul(bank[max_bank(n)], q_stack[0:80, g % SLOTS, at + P * i:at + P * (i + 1)],
                          k_stack[0:80, g % SLOTS, at:at + T], start=True, stop=True).then_inc(S["scores"], 1)

            def values_and_scores(wait, b, ahead, wait_last=None):
                value_products(0)
                value_products(1)
                for n in range(EARLY):
                    if n < 2:
                        qk_product(wait, 2 + n)
                    if n == 2 and wait_last:
                        wait_last("out_made", NT)
                    scores_for_max(b, ahead, n)

            first("tok_normed", NT)
            for j in range(ND):
                turn(0, tok_n, j)
            pe.wait_ge(split_l, ND + 3)
            pe.wait_ge(v_set, 2)
            first("xT_h", ND)
            first("xT_l", ND)
            for n in (0, 1):
                qk_product(first, n)
            values_and_scores(first, 0, 0)
            pe.wait_ge(split_l, ND + len(SPLITS))

            def sequence(b, more):
                wait, wait_next = seq_waits(pe, b), seq_waits(pe, b, 1)

                def turn_max(g):
                    wait("reduced", MG * (g + 1))
                    if g == 1:
                        wait("max_l", 1)
                    elif g >= 2:
                        wait("att_out", g - 1)
                    pe.transpose(bank[7][0:MG, 0:P], row_max[:, g % 2, :], ident[:, :])\
                        .then_inc(S["max_turned"], 1)

                def scoresT_block(s, i):
                    g, kb, n = s // NT, s % NT, GH * s + i
                    if kb == 0 and i == 0:
                        pe.wait_ge(max_in[g], b * 32 + 32)
                    if n >= 3:
                        wait("exped", n - 2 if n < WIDE + 3 else n - 4)
                    if n == WIDE:
                        wait("reduced", NG * MG)
                    pe.matmul(bank[scoresT_bank(n)], k_stack[0:STK, g % SLOTS, T * i + P * kb:T * i + P * (kb + 1)],
                              q_stack[0:STK, g % SLOTS, T * i:T * (i + 1)], start=True, stop=True)\
                        .then_inc(S["scoresT"], 1)

                def weigh_values(s):
                    g, kb = s // NT, s % NT
                    if s == 0:
                        wait("reduced", LEAD)
                    wait("exped", GH * (s + 1))
                    if kb == 0 and g >= 1:
                        wait("attT_made", g)
                    for i in range(GH):
                        last = pe.matmul(bank[6][VW * i:VW * (i + 1), :], v_ext[:, kb, GH * g + i, :],
                                         probs_ring[:, s % PROBS, i, :], start=(kb == 0), stop=(kb == NT - 1))
                    last.then_inc(S["pv_done"], 1)

                def turn_out(g):
                    wait("attT_made", g + 1)
                    if g + 1 < NG:
                        wait("max_l", g + 2)
                    else:
                        wait("att_out", g)
                    for i in range(NT):
                        last = pe.transpose(bank[7][:, P * i:P * (i + 1)], attT[:, P * i:P * (i + 1)], ident[:, :])
                    last.then_inc(S["att_turned"], 1)

                left = iter(range(EARLY, NG * MG))

                def more_scores(count):
                    for n in islice(left, count):
                        scores_for_max(b, 0, n)

                if more:
                    wait_next("onehot_made", 6)
                    for j in range(ND):
                        for part in range(2):
                            if j:
                                wait("qk_l", 3 + part)
                            qg_product(j, part)
                            more_scores(1)
                    for i in range(NT):
                        ev_product(wait_next, i)
                        more_scores(2)
                    mix_product(wait_next, 0)
                    turn_max(0)
                    more_scores(4)
                    mix_product(wait_next, 1)
                    more_scores(LEAD - MG - 5)
                    wait_next("mix_l", ND)
                    wait_next("ev_made", NT)
                else:
                    wait("qk_l", 4)
                    more_scores(MG + 1 - EARLY)
                    turn_max(0)
                    more_scores(LEAD - MG - 1)

                for s in range(STEPS):
                    g, kb = s // NT, s % NT
                    for i in range(GH):
                        scoresT_block(s, i)
                        more_scores(1)
                        if s >= LAST and i == 2:
                            weigh_values(s - 1)
                        if i == 1 and kb == 2 and g + 1 < NG:
                            turn_max(g + 1)
                        if more and i == 1 and ATT_STEP <= s < ATT_STEP + NT:
                            if s == ATT_STEP:
                                wait("reduced", NG * MG)
                            else:
                                wait_next("att_l", s - ATT_STEP)
                            att_product(wait_next, s - ATT_STEP, ATT)
                    if kb == 1 and g >= 1:
                        turn_out(g - 1)
                    if 0 < s < LAST:
                        weigh_values(s - 1)
                    if s == LAST:
                        wait("att_out", 2)
                        if more:
                            wait_next("att_l", NT)
                        turn(1, xn, 0)
                weigh_values(STEPS - 1)

                def project(k, i):
                    for n, (a, c) in enumerate(((0, 0), (0, 1), (1, 0))):
                        last = pe.matmul(bank[i][:, 0:D], xT[a][:, k, P * i:P * (i + 1)], woT[c][:, k, :],
                                         start=(k == 0 and n == 0), stop=(k == ND - 1 and n == 2))
                    return last

                wait("xT_h", ND + 1)
                wait("xT_l", ND + 1)
                for i in range(NT):
                    project(0, i)
                turn_out(NG - 1)
                if more:
                    tok_product(wait_next, 2, TOK)
                wait("att_out", NG)
                turn(1, xn, 1)
                if more:
                    tok_product(wait_next, 3, TOK)
                wait("xT_h", 2 * ND)
                wait("xT_l", 2 * ND)
                for i in range(NT):
                    project(1, i).then_inc(S["proj_sum"], 1)
                if more:
                    for i in (0, 1):
                        tok_product(wait_next, i, TOK)
                    wait_next("tok_made", NT)
                wait("h_normed", 1)
                for j in range(ND):
                    last = pe.transpose(bank[ODD][:, P * j:P * (j + 1)], xn[:, 0, P * j:P * (j + 1)], ident[:, :])
                last.then_inc(S["odd_turned"], 1)

                def broadcast(n):
                    for i in range(2):
                        token = 2 * (2 * n + i) + 1
                        for part in range(2):
                            last = pe.matmul(bank[(6, 7, 0, 1)[n]][:, D * i:D * (i + 1)],
                                             one_r[:, token:token + 1].broadcast_to([P, P]), rows[part],
                                             start=(part == 0), stop=(part == 1))
                    last.then_inc(S["bcast"], 1)

                wait("rows_h", 1)
                wait("rows_l", 1)
                broadcast(0)
                turn(2, xn, 0, lambda i: i and wait("rest_normed", i))
                turn(2, xn, 1)
                broadcast(1)
                broadcast(2)
                broadcast(3)
                wait("xT_h", 3 * ND)
                wait("xT_l", 3 * ND)

                def up(k):
                    if k % 2 == 0:
                        wait("w1_h", k // 2 + 1)
                        wait("w1_l", k // 2 + 1)
                    if k >= 4:
                        wait("gelu_made", k - 3)
                    split_product(bank[UP[k % 4]], lambda a, j: w1_now[a][:, j, P * k:P * (k + 1)],
                                  lambda c, j: xT[c][:, j, :], ND).then_inc(S["hid_sum"], 1)

                AHEAD = 4
                for k in range(AHEAD):
                    up(k)
                for k in range(NH):
                    if k < ND:
                        wait("w2_h", k + 1)
                        wait("w2_l", k + 1)
                    if k == 0:
                        wait("w1_made", 4)
                        wait("w2_made", ND)
                    wait("hid_h", k + 1)
                    wait("hid_l", k + 1)
                    for i in range(NT):
                        for n, (a, c) in enumerate(((0, 0), (0, 1), (1, 0))):
                            last = pe.matmul(bank[SUM[i]][:, 0:D],
                                             hidT[a][:, k % RING, P * i:P * (i + 1)], w2_now[c][:, k, :],
                                             start=(k == 0 and n == 0), stop=(k == NH - 1 and n == 2))
                    last.then_inc(S["hid_used"], 1)
                    if k + AHEAD < NH:
                        up(k + AHEAD)
                    if more and k == 3:
                        wait_next("tok_normed", NT)
                        wait("gelu_made", 6)
                        for j in range(ND):
                            turn(0, tok_n, j)
                    if more and k == 5:
                        wait("gelu_made", NH)
                        wait_next("xT_h", ND)
                        wait_next("xT_l", ND)
                        for n in (0, 1):
                            qk_product(wait_next, n)
                if more:
                    values_and_scores(wait_next, b, 1, wait)

            with pe.Fori(0, B - 1) as b:
                sequence(b, True)
            sequence(B - 1, False)


def _layouts(x, tok_v, tok_Wk, tok_Wq, tok_Wv, qkv_w, qkv_b, out_w, out_b, W1, b1, W2, b2, scale):
    idx = np.concatenate([np.asarray(x), np.asarray(x)[:1]])
    qkv_w, qkv_b = np.asarray(qkv_w), np.asarray(qkv_b)
    order = [part * D + (g * GH + hd) * HD + d
             for part in range(2) for g in range(NG) for d in range(HD) for hd in range(GH)]
    rows = np.concatenate([qkv_w[order], qkv_w[2 * D:]])
    return {
        "idx": idx,
        "idx_cols": idx.reshape(B + 1, NT, P)[:, :, ::-1].transpose(2, 0, 1).reshape(P, (B + 1) * NT),
        "v_pad": np.concatenate([np.zeros(P - 1, np.float32), np.asarray(tok_v)[:, 0]]),
        "wq": np.asarray(tok_Wq), "wk": np.asarray(tok_Wk), "wvT": np.asarray(tok_Wv).T,
        "wqkvT": rows.T,
        "qk_bias": qkv_b[order].reshape(4, P).T, "v_bias": qkv_b[2 * D:],
        "woT": np.asarray(out_w).T, "out_bias": np.asarray(out_b),
        "w1T": np.asarray(W1).T.reshape(ND, P, HID).transpose(1, 0, 2), "b1_col": np.asarray(b1).reshape(NH, P).T,
        "w2T": np.asarray(W2).T.reshape(NH, P, D).transpose(1, 0, 2),
        "b2": np.asarray(b2), "scale": np.asarray(scale).reshape(1),
    }


def kernel(**inputs):
    import concourse.bacc as _bacc
    from concourse.bass_utils import run_bass_kernel_spmd as _run

    names = ["x", "L0_tok_v", "L0_tok_Wk", "L0_tok_Wq", "L0_tok_Wv", "L0_attn_qkv_w", "L0_attn_qkv_b",
             "L0_attn_out_w", "L0_attn_out_b", "L0_ffn_W1", "L0_ffn_b1", "L0_ffn_W2", "L0_ffn_b2", "L0_ffn_scale"]
    laid = _layouts(*(inputs[n] for n in names))
    nc = _bacc.Bacc("TRN2", target_bir_lowering=False, num_devices=1)
    arrays, A = {}, {}
    for name, a in laid.items():
        a = np.ascontiguousarray(a)
        arrays[f"in_{name}_dram"] = a
        A[name] = nc.dram_tensor(f"in_{name}_dram", a.shape, mybir.dt.from_np(a.dtype), kind="ExternalInput").ap()
    A["out"] = nc.dram_tensor("out_dram", (B, T, D), F32, kind="ExternalOutput").ap()
    tower_kernel(nc, A)
    r = _run(nc, [arrays], core_ids=[0])
    return r.results[0]["out_dram"]
```
